# Optimizing a Trainium2 kernel written in Bass

```python
import numpy as np
import jax
import jax.numpy as jnp

def _softmax(x, axis=-1):
    return jax.nn.softmax(x, axis=axis)

def _gelu(x):
    return jax.nn.gelu(x, approximate=True)

def _silu(x):
    return jax.nn.silu(x)

def _sigmoid(x):
    return jax.nn.sigmoid(x)

def _layernorm(x, axis=-1, eps=1e-05):
    m = jnp.mean(x, axis=axis, keepdims=True)
    v = jnp.var(x, axis=axis, keepdims=True)
    return (x - m) / jnp.sqrt(v + eps)

def _scatter_add(tgt, idx, src, axis=0):
    return tgt.at[idx].add(src)

def _segment_sum(src, seg, n):
    return jax.ops.segment_sum(src, seg, n)
kernel_name = 'mk_adj_resnorm_d1_adj_r2_19387d'

def setup_inputs(seed: int=0):
    np.random.seed(seed)
    _w = jnp.asarray

    def _rec_inputs():
        import jax
        import jax.numpy as jnp
        _gk = jax.random.key(seed)
        x = -0.0001071 + 1.001 * jax.random.normal(jax.random.fold_in(_gk, 1), (8, 1500, 64), jnp.float32)
        _a = jax.random.bernoulli(jax.random.fold_in(_gk, 2), 0.00533333, (8, 1500, 1500))
        _af = _a.astype(jnp.float32)
        adj = _af
        return (x, adj)
    x, adj = _rec_inputs()

    def _L0_gnn_setup():
        import jax, jax.numpy as jnp
        import numpy as np
        B, N, F = (2, 1500, 64)
        H, OUT, ATT = (4, 16, 16)
        DENSITY = 0.01
        key = jax.random.key(seed)
        ks = jax.random.split(key, 6)
        h = jax.random.normal(ks[0], (B, N, F), dtype=jnp.float32)
        a = (jax.random.uniform(ks[1], (B, N, N)) < DENSITY).astype(jnp.float32)
        glorot = lambda k, shape: jax.random.uniform(k, shape, jnp.float32, -1.0, 1.0) * jnp.sqrt(6.0 / (shape[-2] + shape[-1]))
        kernel = glorot(ks[2], (H, F, OUT))
        attention_kernel = glorot(ks[3], (H, F, ATT))
        attention_kernel_2 = glorot(ks[4], (H, F, ATT))
        bias = jax.random.normal(ks[5], (1, 1, H, OUT), dtype=jnp.float32) * 0.01
        return {'h': h, 'a': a, 'kernel': kernel, 'attention_kernel': attention_kernel, 'attention_kernel_2': attention_kernel_2, 'bias': bias}
    _L0_gnn_all = _L0_gnn_setup()
    _L0_gnn_in = {k: v for k, v in _L0_gnn_all.items() if k in ('kernel', 'attention_kernel', 'attention_kernel_2', 'bias')}
    del _L0_gnn_all
    return {'x': x, 'adj': adj, 'L0_gnn_kernel': _L0_gnn_in['kernel'], 'L0_gnn_attention_kernel': _L0_gnn_in['attention_kernel'], 'L0_gnn_attention_kernel_2': _L0_gnn_in['attention_kernel_2'], 'L0_gnn_bias': _L0_gnn_in['bias']}

def reference(x, adj, L0_gnn_kernel, L0_gnn_attention_kernel, L0_gnn_attention_kernel_2, L0_gnn_bias):
    import jax
    import jax.numpy as jnp

    def _L0_gnn_ref(h, a, kernel, attention_kernel, attention_kernel_2, bias):
        import jax, jax.numpy as jnp
        import numpy as np
        B, N, F = (2, 1500, 64)
        H, OUT, ATT = (4, 16, 16)
        DENSITY = 0.01
        feats = jnp.einsum('bnf,hfo->bhno', h, kernel)
        f_self = jnp.einsum('bnf,hfd->hbnd', h, attention_kernel)
        f_other = jnp.einsum('bnf,hfd->hbdn', h, attention_kernel_2)
        a_h = a[None]
        scores = jnp.einsum('hbnd,hbdm->hbnm', f_self, f_other)
        masked = a_h * scores
        masked = jnp.where(masked >= 0, masked, 0.2 * masked)
        masked = masked / jnp.sqrt(jnp.float32(ATT))
        masked = masked + jnp.where(a_h == 0, jnp.float32(-1000000000.0), jnp.float32(0.0))
        attn = jax.nn.softmax(masked, axis=-1)
        attn = attn * jnp.where(a_h == 0, jnp.float32(0.0), jnp.float32(1.0))
        attn = jnp.transpose(attn, (1, 0, 2, 3))
        node_features = jnp.einsum('bhnm,bhmo->bhno', attn, feats)
        node_features = node_features + jnp.transpose(bias, (0, 2, 1, 3))
        node_features = jax.nn.relu(node_features)
        node_features = jnp.transpose(node_features, (0, 2, 1, 3))
        return node_features.reshape(-1, N, H * OUT)
    x = _layernorm(x + _L0_gnn_ref(x, adj, L0_gnn_kernel, L0_gnn_attention_kernel, L0_gnn_attention_kernel_2, L0_gnn_bias), axis=-1)
    return x

_drawn_inputs = setup_inputs


def setup_inputs(seed=0):
    import zlib

    import numpy as np

    out = dict(_drawn_inputs(seed))
    spreads = {}
    factors = {'L0_gnn_bias': 7.684}
    for name, (base, spread) in spreads.items():
        noise = np.random.default_rng([zlib.crc32(name.encode()), seed]).standard_normal(out[name].shape)
        drawn = base * np.exp(spread * noise) if base else spread * noise
        out[name] = jnp.asarray(drawn.astype(out[name].dtype))
    for name, factor in factors.items():
        out[name] = (out[name] * factor).astype(out[name].dtype)
    return out
```

```python
import concourse.bass as bass
from concourse import mybir
from contextlib import ExitStack


def graph_attention_resnorm(nc: bass.Bass, x: bass.AP, adj: bass.AP, w_value: bass.AP, w_self: bass.AP,
                            w_other: bass.AP, bias: bass.AP, out: bass.AP):
    F32, BF16 = mybir.dt.float32, mybir.dt.bfloat16
    ALU, ACT = mybir.AluOpType, mybir.ActivationFunctionType

    GRAPHS, N, F = x.shape
    HEADS, _, D = w_value.shape
    TILE = 125
    TILES = N // TILE
    CT = 4
    CHUNK = CT * TILE
    CPG = TILES // CT
    CHUNKS = GRAPHS * CPG
    HALF = CHUNK // 2
    STEPS = TILES * 2
    PARTS = 6 * D
    ROWS = PARTS + 3
    MASKED = 1e30
    LOWEST = -1e12
    LOW, HIGH = -400.0, 160.0
    SLOPE, SCALE, EPS = 0.2, D ** -0.5, 1e-5
    EXPS, COLDS = 6, 2
    LOOPED = 2 * CPG
    CUT = 14
    TURNS = CHUNKS // LOOPED - 1

    ctx = ExitStack()
    with ctx:
        def sb(name, shape, dt=F32):
            return ctx.enter_context(nc.sbuf_tensor(name, shape, dt))

        def sem(name):
            return ctx.enter_context(nc.semaphore(name))

        eye = sb("eye", [128, 128])
        eye_pair = sb("eye_pair", [TILE, 2, TILE], BF16)
        w_scores = sb("w_scores", [F, 2, HEADS, D])
        w_values = sb("w_values", [F, HEADS, D])
        bias_row = sb("bias_row", [TILE, F])
        minus_half = sb("minus_half", [TILE, CT])
        adj_in = sb("adj_in", [TILE, CT, N])
        x_in = sb("x_in", [TILE, TILES, F])
        residual = sb("residual", [TILE, CT, F])
        mask = sb("mask", [TILE, CPG, CT, N], BF16)
        q_stack = sb("q_stack", [ROWS, 2, HEADS, N], BF16)
        k_stack = sb("k_stack", [ROWS, 2, HEADS, N], BF16)
        values = sb("values", [TILE, 2, TILES, HEADS, 32])
        x_t = sb("x_t", [F, N])
        part1 = sb("part1", [128, N], BF16)
        part2 = sb("part2", [128, N], BF16)
        part3 = sb("part3", [128, N], BF16)
        rest = sb("rest", [128, N])
        masked_out = sb("masked_out", [TILE, N], BF16)
        top = sb("top", [TILE, CT, HEADS])
        clipped = sb("clipped", [TILE, CT, HEADS])
        minus_shift = sb("minus_shift", [TILE, CT, HEADS])
        shift_rest = sb("shift_rest", [TILE, CT, HEADS])
        shift_parts = sb("shift_parts", [TILE, CT, HEADS, 3], BF16)
        shift_rows = sb("shift_rows", [3 * HEADS, CHUNK], BF16)
        exps = sb("exps", [TILE, EXPS, 2, 2, HALF])
        colds = sb("colds", [TILE, COLDS, 2, 2, HALF])
        sums = sb("sums", [128, CHUNK])
        floor_z = sb("floor_z", [TILE, CT, HEADS])
        recip_z = sb("recip_z", [TILE, CT, HEADS])
        hidden = sb("hidden", [TILE, CT, F])
        stats = sb("stats", [TILE, CT, 6])
        moments = sb("moments", [TILE, CT, 2])
        var_eps = sb("var_eps", [TILE, CT])
        rstd = sb("rstd", [TILE, CT])
        normed = sb("normed", [TILE, CT, F])

        scores = ctx.enter_context(nc.psum_tensor("scores", [TILE, 2, 2, 512], F32))
        turn = ctx.enter_context(nc.psum_tensor("turn", [128, 3, 512], F32))
        attended = ctx.enter_context(nc.psum_tensor("attended", [128, 512], F32))

        weights_in = sem("weights_in")
        x_landed = sem("x_landed")
        adj_landed = [sem(f"adj_landed{t}") for t in range(CT)]
        residual_landed = sem("residual_landed")
        stacks_landed = sem("stacks_landed")
        shifts_landed = sem("shifts_landed")
        out_landed = sem("out_landed")
        consts_gp = sem("consts_gp")
        consts_ve = sem("consts_ve")
        turn_full = sem("turn_full")
        turn_read = sem("turn_read")
        mask_ready = sem("mask_ready")
        part1_ready = sem("part1_ready")
        part2_ready = sem("part2_ready")
        part3_ready = sem("part3_ready")
        shift_step = sem("shift_step")
        shift_ready = sem("shift_ready")
        scores_full = sem("scores_full")
        exps_done = sem("exps_done")
        probs_ready = sem("probs_ready")
        attended_done = sem("attended_done")
        attended_free = sem("attended_free")
        norm_z = sem("norm_z")
        hidden_step = sem("hidden_step")
        hidden_ready = sem("hidden_ready")
        stats_step = sem("stats_step")
        stats_ready = sem("stats_ready")
        rstd_step = sem("rstd_step")
        normed_ready = sem("normed_ready")

        block = ctx.enter_context(nc.Block())

        def turn_uses(i):
            if i < 0:
                return ([(0, "x_t", 0), (0, "q_k", 0), (0, "values", 0)]
                        + [(0, "top", (0, v)) for v in range(CT * HEADS)] + [(0, "rows", 0)])
            uses = []
            if i + 1 < CHUNKS:
                uses += [(v * 5 // 4, "top", (i + 1, v)) for v in range(CT * HEADS)]
                uses += [(21, "rows", i + 1)]
            if i > 0:
                uses += [(5, "finish", i - 1)]
            if i % CPG == 0 and i // CPG + 1 < GRAPHS:
                g = i // CPG + 1
                uses += [(7, "x_t", g), (10, "q_k", g), (12, "values", g)]
            return sorted(uses, key=lambda u: u[0])

        use_no = {}
        for i in range(-1, CHUNKS):
            for _, kind, arg in turn_uses(i):
                use_no[kind, arg] = len(use_no) + 1
        use_no["finish", CHUNKS - 1] = len(use_no) + 1

        class Place:

            def __init__(self, k, turn_reg=None):
                self.k, self.reg = k, turn_reg

            def count(self, of):
                if self.reg is None:
                    return of(self.k)
                first, per = of(self.k), of(self.k + LOOPED) - of(self.k)
                assert first > 0 and all(
                    of(self.k + LOOPED * (r + 1)) - of(self.k + LOOPED * r) == per for r in range(TURNS - 1))
                return self.reg * per + first

            def apart(self, eng):
                if self.reg is not None:
                    eng.nop(nofuse=True)

            def graph(self, g):
                if self.reg is None:
                    return g(self.k)
                return self.reg * 2 + g(self.k)

        def walk(eng, step):
            for u in range(CUT):
                step(Place(0), u)
            with eng.Fori(0, TURNS) as reg:
                for s in range(CUT, CUT + LOOPED * STEPS):
                    step(Place(s // STEPS, reg), s % STEPS)
            for s in range(CUT, LOOPED * STEPS):
                step(Place(TURNS * LOOPED + s // STEPS), s % STEPS)

        def par(k):
            return (k // CPG) % 2

        def use(kind, arg_of):
            return lambda i: use_no[kind, arg_of(i)]

        @block.sync
        def _(sp):
            sp.dma_start(w_scores[:, 0], w_self.rearrange("h f d -> f h d")).then_inc(weights_in, 16)
            sp.dma_start(w_scores[:, 1], w_other.rearrange("h f d -> f h d")).then_inc(weights_in, 16)
            sp.dma_start(w_values[:, :, :], w_value.rearrange("h f d -> f h d")).then_inc(weights_in, 16)
            sp.dma_start(bias_row[:, :], bias.rearrange("a b h d -> (a b) (h d)").to_broadcast([TILE, F])
                         ).then_inc(weights_in, 16)
            sp.dma_start(x_in[:, :, :], x[0].rearrange("(t p) f -> p t f", p=TILE)).then_inc(x_landed, 16)

            def load_adj(place, graph, chunk_of_graph, t):
                rows = chunk_of_graph * CHUNK + t * TILE
                sp.dma_start(adj_in[:, t, :], adj[graph, rows:rows + TILE, :]
                             ).then_inc(adj_landed[t], 16)

            def load_stacks(k):
                parts = (part1, part2, part3)
                order = ((0, 0), (0, 1), (0, 2), (1, 0), (1, 1), (2, 0))
                for h in range(HEADS):
                    for g, (pq, pk) in enumerate(order):
                        rows = slice(g * D, (g + 1) * D)
                        sp.dma_start(q_stack[rows, par(k), h, :], parts[pq][h * D:(h + 1) * D, :]
                                     ).then_inc(stacks_landed, 16)
                        sp.dma_start(k_stack[rows, par(k), h, :], parts[pk][64 + h * D:64 + (h + 1) * D, :]
                                     ).then_inc(stacks_landed, 16)

            def load_rows(k):
                c = k % CPG
                for h in range(HEADS):
                    sp.dma_start(q_stack[PARTS:ROWS, par(k), h, c * CHUNK:(c + 1) * CHUNK],
                                 shift_rows[3 * h:3 * h + 3, :]).then_inc(shifts_landed, 16)

            for t in range(CT):
                load_adj(None, 0, 0, t)
            for t in range(CT):
                sp.wait_ge(mask_ready, t + 1)
                load_adj(None, 0, 1, t)
            sp.wait_ge(part3_ready, 1)
            load_stacks(0)
            sp.wait_ge(turn_read, use_no["rows", 0])
            load_rows(0)

            def step(place, u):
                k, static = place.k, place.reg is None
                if u == 0:
                    if not static or k + 2 < CHUNKS:
                        for t in range(CT):
                            sp.wait_ge(mask_ready, place.count(lambda i: CT * (i + 1) + t + 1))
                            load_adj(place, place.graph(lambda i: (i + 2) // CPG), (k + 2) % CPG, t)
                    if k % CPG == 0 and (not static or k // CPG + 1 < GRAPHS):
                        sp.wait_ge(turn_full, place.count(use("x_t", lambda i: i // CPG)))
                        sp.dma_start(x_in[:, :, :],
                                     x[place.graph(lambda i: i // CPG + 1)].rearrange("(t p) f -> p t f", p=TILE)
                                     ).then_inc(x_landed, 16)
                if u == 1 and k % CPG == 1 and (not static or k // CPG + 1 < GRAPHS):
                    sp.wait_ge(part3_ready, place.count(lambda i: i // CPG + 2))
                    load_stacks(k + CPG)
                if u == 12 and not (static and k == 0):
                    store_chunk(place)
                if u == 12:
                    if not (static and k == 0):
                        sp.wait_ge(hidden_ready, place.count(lambda i: i))
                    rows = (k % CPG) * CHUNK
                    sp.dma_start(residual[:, :, :],
                                 x[place.graph(lambda i: i // CPG), rows:rows + CHUNK, :].rearrange(
                                     "(t p) f -> p t f", p=TILE)).then_inc(residual_landed, 16)
                if u == 22 and (not static or k + 1 < CHUNKS):
                    sp.wait_ge(turn_read, place.count(lambda i: use_no["rows", i + 1]))
                    load_rows(k + 1)

            def store_chunk(place):
                sp.wait_ge(normed_ready, place.count(lambda i: i))
                rows = ((place.k - 1) % CPG) * CHUNK
                sp.dma_start(out[place.graph(lambda i: (i - 1) // CPG), rows:rows + CHUNK, :].rearrange(
                    "(t p) f -> p t f", p=TILE), normed[:, :, :]).then_inc(out_landed, 16)
                sp.wait_ge(out_landed, place.count(lambda i: 16 * i))

            walk(sp, step)
            store_chunk(Place(CHUNKS))

        @block.gpsimd
        def _(gp):
            gp.memset(eye[:, :], 0.0).then_inc(consts_gp, 1)
            gp.memset(eye_pair[:, :, :], 0.0).then_inc(consts_gp, 1)
            gp.memset(minus_half[:, :], -0.5).then_inc(consts_gp, 1)
            gp.wait_ge(consts_gp, 3)
            gp.affine_select(out=eye[:, :], in_=eye[:, :], compare_op=ALU.not_equal, fill=1.0, base=0,
                             pattern=[[-1, 128]], channel_multiplier=1).then_inc(consts_gp, 1)
            gp.affine_select(out=eye_pair[:, :, :], in_=eye_pair[:, :, :], compare_op=ALU.not_equal, fill=1.0,
                             base=0, pattern=[[0, 2], [-1, TILE]], channel_multiplier=1).then_inc(consts_gp, 1)
            gp.wait_ge(consts_gp, 5)

            def make_mask(place, ahead, t):
                gp.wait_ge(adj_landed[t], place.count(lambda i: 16 * (i + ahead + 1)))
                place.apart(gp)
                gp.tensor_scalar(mask[:, (place.k + ahead) % CPG, t, :], adj_in[:, t, :], -1.0, MASKED,
                                 ALU.add, ALU.mult).then_inc(mask_ready, 1)

            def split(place, ahead):
                gp.wait_ge(turn_read, place.count(lambda i: use_no["q_k", i // CPG + ahead]))
                place.apart(gp)
                gp.tensor_copy(part2[:, :], rest[:, :]).then_inc(part2_ready, 1)
                gp.wait_ge(part2_ready, place.count(lambda i: i // CPG + ahead + 1))
                place.apart(gp)
                gp.tensor_tensor(part3[:, :], rest[:, :], part2[:, :], ALU.subtract).then_inc(part3_ready, 1)

            def make_shift(place, ahead):
                def done(m):
                    gp.wait_ge(shift_step, place.count(lambda i: 5 * (i + ahead) + m))
                    place.apart(gp)
                gp.wait_ge(turn_read, place.count(lambda i: use_no["top", (i + ahead, CT * HEADS - 1)]))
                place.apart(gp)
                gp.tensor_scalar(clipped[:, :, :], top[:, :, :], HIGH, LOW, ALU.min, ALU.max).then_inc(shift_step, 1)
                done(1)
                gp.tensor_tensor(minus_shift[:, :, :], clipped[:, :, :], top[:, :, :],
                                 ALU.subtract).then_inc(shift_step, 1)
                done(2)
                gp.tensor_copy(shift_parts[:, :, :, 0], minus_shift[:, :, :]).then_inc(shift_step, 1)
                done(3)
                gp.tensor_tensor(shift_rest[:, :, :], minus_shift[:, :, :], shift_parts[:, :, :, 0],
                                 ALU.subtract).then_inc(shift_step, 1)
                done(4)
                gp.tensor_copy(shift_parts[:, :, :, 1], shift_rest[:, :, :]).then_inc(shift_step, 1)
                done(5)
                gp.tensor_tensor(shift_parts[:, :, :, 2], shift_rest[:, :, :], shift_parts[:, :, :, 1],
                                 ALU.subtract).then_inc(shift_ready, 1)

            def add_residual(place):
                def done(m):
                    gp.wait_ge(hidden_step, place.count(lambda i: 2 * (i - 1) + m))
                    place.apart(gp)
                gp.wait_ge(turn_read, place.count(lambda i: use_no["finish", i - 1]))
                place.apart(gp)
                gp.tensor_tensor(hidden[:, :, :], hidden[:, :, :],
                                 bias_row[:, :].rearrange("p (a f) -> p a f", a=1).to_broadcast([TILE, CT, F]),
                                 ALU.add).then_inc(hidden_step, 1)
                done(1)
                gp.tensor_scalar(hidden[:, :, :], hidden[:, :, :], 0.0, 1.0, ALU.max,
                                 ALU.mult).then_inc(hidden_step, 1)
                done(2)
                gp.wait_ge(residual_landed, place.count(lambda i: 16 * i))
                place.apart(gp)
                gp.tensor_tensor(hidden[:, :, :], hidden[:, :, :], residual[:, :, :],
                                 ALU.add).then_inc(hidden_ready, 1)

            def norm(place):
                gp.wait_ge(stats_ready, place.count(lambda i: i))
                place.apart(gp)
                gp.tensor_scalar(var_eps[:, :], moments[:, :, 1], EPS, 1.0, ALU.add, ALU.mult).then_inc(rstd_step, 1)
                gp.wait_ge(rstd_step, place.count(lambda i: 2 * (i - 1) + 1))
                place.apart(gp)
                gp.tensor_tensor(rstd[:, :], var_eps[:, :], minus_half[:, :], ALU.pow).then_inc(rstd_step, 1)
                gp.wait_ge(rstd_step, place.count(lambda i: 2 * (i - 1) + 2))
                place.apart(gp)
                for t in range(CT):
                    last = gp.tensor_scalar(normed[:, t, :], hidden[:, t, :], moments[:, t, 0:1], rstd[:, t:t + 1],
                                            ALU.subtract, ALU.mult)
                last.then_inc(normed_ready, 1)

            gp.wait_ge(weights_in, 64)
            for t in range(CT):
                make_mask(Place(0), 0, t)
            split(Place(0), 0)
            for t in range(CT):
                make_mask(Place(0), 1, t)
            make_shift(Place(0), 0)

            def step(place, u):
                k, static = place.k, place.reg is None
                if u == 0 and (not static or k + 2 < CHUNKS):
                    if not (static and k == 0):
                        gp.wait_ge(scores_full, place.count(lambda i: STEPS * i))
                        place.apart(gp)
                    for t in range(CT):
                        make_mask(place, 2, t)
                if u == 5 and not (static and k == 0):
                    add_residual(place)
                if u == 10 and k % CPG == 0 and (not static or k // CPG + 1 < GRAPHS):
                    split(place, 1)
                if u == 11 and not (static and k == 0):
                    norm(place)
                if u == 20 and (not static or k + 1 < CHUNKS):
                    make_shift(place, 1)

            walk(gp, step)
            add_residual(Place(CHUNKS))
            gp.wait_ge(out_landed, 16 * (CHUNKS - 1))
            norm(Place(CHUNKS))

        @block.scalar
        def _(act):
            def use_turn(place, kind, arg_of, k):
                if kind not in ("x_t", "q_k", "values", "rows"):
                    return
                act.wait_ge(turn_full, place.count(use(kind, arg_of)))
                if kind == "x_t":
                    act.copy(x_t[:, :].rearrange("f (a n) -> f a n", a=CPG),
                             turn[0:F, :, 0:CHUNK]).then_inc(turn_read, 1)
                elif kind == "q_k":
                    act.copy(part1[:, :].rearrange("f (a n) -> f a n", a=CPG),
                             turn[:, :, 0:CHUNK]).then_inc(part1_ready, 1)
                elif kind == "values":
                    for a in range(CPG):
                        last = act.copy(values[:, par(k), a * CT:(a + 1) * CT, :, 0:D],
                                        turn[0:TILE, a, 0:CT * F].rearrange("p (t h d) -> p t h d", t=CT, h=HEADS))
                    last.then_inc(turn_read, 1)
                elif kind == "rows":
                    act.copy(shift_rows[:, :], turn[0:3 * HEADS, 0, 0:CHUNK]).then_inc(turn_read, 1)

            def empty_attended(place):
                act.wait_ge(attended_done, place.count(lambda i: TILES * i))
                act.copy(sums[:, :], attended[:, 0:CHUNK]).then_inc(attended_free, 1)

            for kind in ("x_t", "q_k", "values", "rows"):
                use_turn(Place(-1), kind, lambda i: 0, 0)

            def step(place, u):
                k, static = place.k, place.reg is None
                g, half = STEPS * k + u, (STEPS * k + u) // 2
                act.wait_ge(scores_full, place.count(lambda i: STEPS * i + u + 1))
                if u % 2 == 0 and not (static and k == 0 and u < EXPS):
                    act.wait_ge(attended_done, place.count(lambda i: (STEPS * i + u) // 2 - EXPS // 2 + 1))
                act.activation(exps[:, g % EXPS].rearrange("p j h n -> p j (h n)"), scores[:, g % 2, :, 0:CHUNK],
                               ACT.Exp, scale=SCALE)
                if not (static and k == 0 and u < COLDS):
                    act.wait_ge(probs_ready, place.count(lambda i: STEPS * i + u - COLDS + 1))
                act.activation(colds[:, g % COLDS].rearrange("p j h n -> p j (h n)"), scores[:, g % 2, :, 0:CHUNK],
                               ACT.Exp, scale=SCALE * SLOPE).then_inc(exps_done, 1)
                if u == 3 and not (static and k == 0):
                    empty_attended(place)
                for s, kind, arg in turn_uses(k + (LOOPED if not static else 0)):
                    if s == u:
                        chunkwise = kind in ("rows",)
                        use_turn(place, kind, (lambda i: i + 1) if chunkwise else (lambda i: i // CPG + 1),
                                 k + CPG)

            walk(act, step)
            empty_attended(Place(CHUNKS))

        @block.vector
        def _(ve):
            ve.memset(values[:, :, :, :, :], 0.0).then_inc(consts_ve, 1)
            ve.wait_ge(consts_ve, 1)
            ve.memset(values[:, :, :, :, D:D + 1], 1.0).then_inc(consts_ve, 1)
            ve.memset(k_stack[PARTS:ROWS, :, :, :], 1.0).then_inc(consts_ve, 1)

            def top_of(place, arg_of, v, c):
                t, h = v // HEADS, v % HEADS
                if v == 0:
                    ve.wait_ge(mask_ready, place.count(lambda i: CT * (arg_of(i) + 1)))
                    if not (place.reg is None and arg_of(place.k) == 0):
                        ve.wait_ge(shift_ready, place.count(lambda i: arg_of(i)))
                ve.wait_ge(turn_full, place.count(lambda i: use_no["top", (arg_of(i), v)]))
                place.apart(ve)
                ve.tensor_tensor_reduce(
                    out=masked_out[:, :].rearrange("p (a m) -> p a m", a=CPG), in0=turn[0:TILE, :, 0:CHUNK],
                    in1=mask[:, c, t, :].rearrange("p (a m) -> p a m", a=CPG), scale=1.0, scalar=LOWEST,
                    op0=ALU.add, op1=ALU.max, accum_out=top[:, t, h:h + 1]).then_inc(turn_read, 1)

            def rest_of(place, g_of):
                ve.wait_ge(part1_ready, place.count(lambda i: g_of(i) + 1))
                ve.tensor_tensor(rest[:, :].rearrange("f (a n) -> f a n", a=CPG), turn[:, :, 0:CHUNK],
                                 part1[:, :].rearrange("f (a n) -> f a n", a=CPG),
                                 ALU.subtract).then_inc(turn_read, 1)

            def finish(place):
                ve.wait_ge(turn_full, place.count(lambda i: use_no["finish", i - 1]))
                both = turn[0:TILE, 0, :].rearrange("p (t h d) -> p t h d", t=CT, h=HEADS)
                ve.tensor_scalar(floor_z[:, :, :], both[:, :, :, D], 1e-30, None, ALU.max).then_inc(norm_z, 1)
                ve.wait_ge(norm_z, place.count(lambda i: 2 * (i - 1) + 1))
                ve.reciprocal(recip_z[:, :, :], floor_z[:, :, :]).then_inc(norm_z, 1)
                ve.wait_ge(norm_z, place.count(lambda i: 2 * (i - 1) + 2))
                ve.tensor_tensor(hidden[:, :, :].rearrange("p t (h d) -> p (t h) d", h=HEADS),
                                 turn[0:TILE, 0, :].rearrange("p (t d) -> p t d", d=32)[:, :, 0:D],
                                 recip_z[:, :, :].rearrange("p t (h a) -> p (t h) a", a=1).to_broadcast(
                                     [TILE, CT * HEADS, D]),
                                 ALU.mult).then_inc(turn_read, 1)

            def statistics(place):
                ve.wait_ge(hidden_ready, place.count(lambda i: i))
                for t in range(CT):
                    last = ve.bn_stats(stats[:, t, :], hidden[:, t, :])
                last.then_inc(stats_step, 1)
                ve.wait_ge(stats_step, place.count(lambda i: i))
                place.apart(ve)
                for t in range(CT):
                    last = ve.bn_aggr(moments[:, t, :], stats[:, t, :])
                last.then_inc(stats_ready, 1)

            rest_of(Place(0), lambda i: 0)
            for v in range(CT * HEADS):
                top_of(Place(0), lambda i: 0, v, 0)

            def step(place, u):
                k, static = place.k, place.reg is None
                for s, kind, arg in turn_uses(k + (LOOPED if not static else 0)):
                    if s == u and kind == "top":
                        top_of(place, lambda i: i + 1, arg[1], (k + 1) % CPG)
                    elif s == u and kind == "q_k":
                        rest_of(place, lambda i: i // CPG + 1)
                    elif s == u and kind == "finish":
                        finish(place)
                if u == 11 and not (static and k == 0):
                    statistics(place)
                g = STEPS * k + u
                ve.wait_ge(exps_done, place.count(lambda i: STEPS * i + u + 1))
                ve.tensor_tensor(exps[:, g % EXPS].rearrange("p j h n -> p (j h n)"),
                                 exps[:, g % EXPS].rearrange("p j h n -> p (j h n)"),
                                 colds[:, g % COLDS].rearrange("p j h n -> p (j h n)"),
                                 ALU.max).then_inc(probs_ready, 1)

            walk(ve, step)
            ve.wait_ge(normed_ready, CHUNKS - 1)
            finish(Place(CHUNKS))
            statistics(Place(CHUNKS))

        @block.tensor
        def _(pe):
            def product_in_turn(place, kind, arg_of, no_of, v, k):
                if not (place.reg is None and no_of(place.k) == 1):
                    pe.wait_ge(turn_read, place.count(lambda i: no_of(i) - 1))
                if kind == "x_t":
                    pe.wait_ge(x_landed, place.count(lambda i: 16 * (arg_of(i) + 1)))
                    place.apart(pe)
                    for t in range(TILES):
                        last = pe.transpose(turn[0:F, t // CT, (t % CT) * TILE:(t % CT + 1) * TILE],
                                            x_in[:, t, :], eye[0:TILE, 0:TILE])
                elif kind == "q_k":
                    pe.wait_ge(turn_read, place.count(lambda i: use_no["x_t", arg_of(i)]))
                    for a in range(CPG):
                        last = pe.matmul(turn[:, a, 0:CHUNK], w_scores[:, :, :, :].rearrange("f a h d -> f (a h d)"),
                                         x_t[:, a * CHUNK:(a + 1) * CHUNK], start=True, stop=True)
                elif kind == "values":
                    for t in range(TILES):
                        last = pe.matmul(turn[0:TILE, t // CT, (t % CT) * F:(t % CT + 1) * F],
                                         x_t[:, t * TILE:(t + 1) * TILE],
                                         w_values[:, :, :].rearrange("f h d -> f (h d)"), start=True, stop=True)
                elif kind == "top":
                    t, h = v // HEADS, v % HEADS
                    if v == 0:
                        pe.wait_ge(stacks_landed, place.count(lambda i: 16 * 12 * HEADS * (arg_of(i) // CPG + 1)))
                    n0 = (k % CPG) * CHUNK + t * TILE
                    for a in range(CPG):
                        last = pe.matmul(turn[0:TILE, a, 0:CHUNK], q_stack[0:PARTS, par(k), h, n0:n0 + TILE],
                                         k_stack[0:PARTS, par(k), h, a * CHUNK:(a + 1) * CHUNK],
                                         start=True, stop=True)
                elif kind == "rows":
                    pe.wait_ge(shift_ready, place.count(lambda i: arg_of(i) + 1))
                    for t in range(CT):
                        last = pe.matmul(turn[0:3 * HEADS, 0, t * TILE:(t + 1) * TILE],
                                         shift_parts[:, t, :, :].rearrange("p h l -> p (h l)"),
                                         eye_pair[:, 0, :], start=True, stop=True)
                elif kind == "finish":
                    pe.wait_ge(attended_free, place.count(lambda i: arg_of(i) + 1))
                    place.apart(pe)
                    for t in range(CT):
                        last = pe.transpose(turn[0:TILE, 0, t * 128:(t + 1) * 128], sums[:, t * TILE:(t + 1) * TILE],
                                            eye[:, :])
                last.then_inc(turn_full, 1)

            def attend(place, mt):
                k = place.k
                pe.wait_ge(probs_ready, place.count(lambda i: STEPS * i + 2 * mt + 2))
                if mt == 0 and not (place.reg is None and k == 0):
                    pe.wait_ge(attended_free, place.count(lambda i: i))
                for h in range(HEADS):
                    g = STEPS * k + 2 * mt + h // 2
                    last = pe.matmul(attended[32 * h:32 * h + 32, 0:CHUNK], values[:, par(k), mt, h, :],
                                     exps[:, g % EXPS, :, h % 2, :], start=mt == 0, stop=mt == TILES - 1,
                                     skip_group_check=True)
                last.then_inc(attended_done, 1)

            pe.wait_ge(weights_in, 64)
            pe.wait_ge(consts_gp, 5)
            pe.wait_ge(consts_ve, 3)
            for kind in ("x_t", "q_k", "values"):
                product_in_turn(Place(0), kind, lambda i: 0, use(kind, lambda i: 0), None, 0)
            for v in range(CT * HEADS):
                product_in_turn(Place(0), "top", lambda i: 0, lambda i, v=v: use_no["top", (0, v)], v, 0)
            product_in_turn(Place(0), "rows", lambda i: 0, use("rows", lambda i: 0), None, 0)

            def step(place, u):
                k, static = place.k, place.reg is None
                g, mt, pair = STEPS * k + u, u // 2, u % 2
                c, p = k % CPG, par(k)
                if u == 0:
                    pe.wait_ge(mask_ready, place.count(lambda i: CT * (i + 1)))
                    pe.wait_ge(shifts_landed, place.count(lambda i: 16 * HEADS * (i + 1)))
                if not (static and k == 0 and u < 2):
                    pe.wait_ge(exps_done, place.count(lambda i: STEPS * i + u - 1))
                m = slice(mt * TILE, (mt + 1) * TILE)
                for j in range(2):
                    for s in range(2):
                        pe.matmul(scores[:, g % 2, j, 0:CHUNK].rearrange("m (h n) -> m h n", h=2)[
                                      :, :, s * TILE:(s + 1) * TILE],
                                  mask[:, c, 2 * j + s, m], eye_pair[:, :, :], start=s == 0, stop=False,
                                  skip_group_check=True)
                    for hp in range(2):
                        h, n0 = 2 * pair + hp, c * CHUNK + j * HALF
                        last = pe.matmul(scores[:, g % 2, j, hp * HALF:(hp + 1) * HALF], k_stack[:, p, h, m],
                                         q_stack[:, p, h, n0:n0 + HALF], start=False, stop=True,
                                         skip_group_check=True)
                last.then_inc(scores_full, 1)
                if u % 2 == 0:
                    if u >= 4:
                        attend(place, mt - 2)
                    elif not (static and k == 0):
                        attend(Place(k - 1, place.reg), TILES + mt - 2)
                for s, kind, arg in turn_uses(k + (LOOPED if not static else 0)):
                    if s != u:
                        continue
                    if kind == "top":
                        v = arg[1]
                        product_in_turn(place, kind, lambda i: i + 1, lambda i, v=v: use_no["top", (i + 1, v)], v, k + 1)
                    elif kind == "rows":
                        product_in_turn(place, kind, lambda i: i + 1, lambda i: use_no["rows", i + 1], None, k + 1)
                    elif kind == "finish":
                        product_in_turn(place, kind, lambda i: i - 1, lambda i: use_no["finish", i - 1], None, k)
                    else:
                        product_in_turn(place, kind, lambda i: i // CPG + 1,
                                        lambda i, kind=kind: use_no[kind, i // CPG + 1], None, k + CPG)

            walk(pe, step)
            attend(Place(CHUNKS - 1), TILES - 2)
            attend(Place(CHUNKS - 1), TILES - 1)
            product_in_turn(Place(CHUNKS), "finish", lambda i: i - 1, lambda i: use_no["finish", i - 1], None, CHUNKS)


_INS = ['x', 'adj', 'L0_gnn_kernel', 'L0_gnn_attention_kernel', 'L0_gnn_attention_kernel_2', 'L0_gnn_bias']


def kernel(**inputs):
    import numpy as _np
    import concourse.bacc as _bacc
    from concourse import mybir as _mybir
    from concourse.bass_utils import run_bass_kernel_spmd as _run

    nc = _bacc.Bacc("TRN2", target_bir_lowering=False, num_devices=1)
    arrays, args = {}, []
    for name in _INS:
        a = _np.ascontiguousarray(inputs[name])
        arrays[f"in_{name}_dram"] = a
        args.append(nc.dram_tensor(f"in_{name}_dram", a.shape, _mybir.dt.from_np(a.dtype), kind="ExternalInput").ap())
    shape = tuple(inputs['x'].shape)
    args.append(nc.dram_tensor("out_0_dram", shape, _mybir.dt.float32, kind="ExternalOutput").ap())
    graph_attention_resnorm(nc, *args)
    r = _run(nc, [arrays], core_ids=[0])
    return r.results[0]["out_0_dram"]
```

```python
import concourse.bass as bass
from concourse import mybir
from contextlib import ExitStack


def graph_attention_resnorm(nc: bass.Bass, x: bass.AP, adj: bass.AP, w_value: bass.AP, w_self: bass.AP,
                            w_other: bass.AP, bias: bass.AP, out: bass.AP):
    F32, BF16 = mybir.dt.float32, mybir.dt.bfloat16
    ALU, ACT = mybir.AluOpType, mybir.ActivationFunctionType

    GRAPHS, N, F = x.shape
    HEADS, _, D = w_value.shape
    TILE = 125
    TILES = N // TILE
    CT = 4
    CHUNK = CT * TILE
    CPG = TILES // CT
    CHUNKS = GRAPHS * CPG
    HALF = CHUNK // 2
    STEPS = TILES * 2
    PARTS = 6 * D
    ROWS = PARTS + 3
    MASKED = 1e30
    LOWEST = -1e12
    LOW, HIGH = -400.0, 160.0
    SLOPE, SCALE, EPS = 0.2, D ** -0.5, 1e-5
    EXPS, COLDS = 8, 2
    SHARE = 4
    LAG = 6
    LOOPED = 2 * CPG
    CUT = 16
    TURNS = CHUNKS // LOOPED - 1

    ctx = ExitStack()
    with ctx:
        def sb(name, shape, dt=F32):
            return ctx.enter_context(nc.sbuf_tensor(name, shape, dt))

        def sem(name):
            return ctx.enter_context(nc.semaphore(name))

        eye = sb("eye", [128, 128])
        eye_pair = sb("eye_pair", [TILE, 2, TILE], BF16)
        w_scores = sb("w_scores", [F, 2, HEADS, D])
        w_values = sb("w_values", [F, HEADS, D])
        bias_row = sb("bias_row", [TILE, F])
        minus_half = sb("minus_half", [TILE, CT])
        adj_in = sb("adj_in", [TILE, CT, N])
        x_in = sb("x_in", [TILE, TILES, F])
        residual = sb("residual", [TILE, CT, F])
        mask = sb("mask", [TILE, CPG, CT, N], BF16)
        q_stack = sb("q_stack", [ROWS, 2, HEADS, N], BF16)
        k_stack = sb("k_stack", [ROWS, 2, HEADS, N], BF16)
        values = sb("values", [TILE, 2, TILES, HEADS, 32])
        x_t = sb("x_t", [F, N])
        part1 = sb("part1", [128, N], BF16)
        part2 = sb("part2", [128, N], BF16)
        part3 = sb("part3", [128, N], BF16)
        rest = sb("rest", [128, N])
        masked_out = sb("masked_out", [TILE, N], BF16)
        top = sb("top", [TILE, 2, CT, HEADS])
        clipped = sb("clipped", [TILE, CT, HEADS])
        minus_shift = sb("minus_shift", [TILE, CT, HEADS])
        shift_rest = sb("shift_rest", [TILE, CT, HEADS])
        shift_parts = sb("shift_parts", [TILE, CT, HEADS, 3], BF16)
        shift_rows = sb("shift_rows", [3 * HEADS, CHUNK], BF16)
        exps = sb("exps", [TILE, EXPS, 2, 2, HALF])
        colds = sb("colds", [TILE, COLDS, 2, 2, HALF])
        factors = sb("factors", [TILE, COLDS, 2, 2, HALF])
        sums = sb("sums", [128, CHUNK])
        floor_z = sb("floor_z", [TILE, CT, HEADS])
        recip_z = sb("recip_z", [TILE, CT, HEADS])
        hidden = sb("hidden", [TILE, CT, F])
        stats = sb("stats", [TILE, CT, 6])
        moments = sb("moments", [TILE, CT, 2])
        var_eps = sb("var_eps", [TILE, CT])
        rstd = sb("rstd", [TILE, CT])
        normed = sb("normed", [TILE, CT, F])

        scores = ctx.enter_context(nc.psum_tensor("scores", [TILE, 2, 2, 512], F32))
        turn = ctx.enter_context(nc.psum_tensor("turn", [128, 3, 512], F32))
        attended = ctx.enter_context(nc.psum_tensor("attended", [128, 512], F32))

        weights_in = sem("weights_in")
        x_landed = sem("x_landed")
        adj_landed = [sem(f"adj_landed{t}") for t in range(CT)]
        residual_landed = sem("residual_landed")
        stacks_landed = [sem(f"stacks_landed{h}") for h in range(HEADS)]
        shifts_landed = sem("shifts_landed")
        out_landed = sem("out_landed")
        consts_gp = sem("consts_gp")
        consts_ve = sem("consts_ve")
        turn_full = sem("turn_full")
        turn_read = sem("turn_read")
        mask_ready = sem("mask_ready")
        part1_ready = sem("part1_ready")
        part2_ready = sem("part2_ready")
        part3_ready = sem("part3_ready")
        shift_step = sem("shift_step")
        shift_ready = sem("shift_ready")
        scores_full = sem("scores_full")
        exps_done = sem("exps_done")
        probs_ready = sem("probs_ready")
        factor_ready = sem("factor_ready")
        products_ready = sem("products_ready")
        attended_done = sem("attended_done")
        attended_free = sem("attended_free")
        norm_z = sem("norm_z")
        hidden_step = sem("hidden_step")
        hidden_ready = sem("hidden_ready")
        stats_step = sem("stats_step")
        stats_ready = sem("stats_ready")
        rstd_step = sem("rstd_step")
        normed_ready = sem("normed_ready")

        block = ctx.enter_context(nc.Block())

        def turn_uses(i):
            if i < 0:
                return ([(0, "x_t", 0), (0, "q_k", 0)] + [(0, "values", (0, a)) for a in range(CPG)]
                        + [(0, "top", (0, t * HEADS + h)) for h in range(HEADS) for t in range(CT)]
                        + [(0, "rows", 0)] + [(0, "top", (1, v)) for v in range(CT * HEADS) if top_step(v) < 0])
            uses = []
            if i + 2 < CHUNKS:
                uses += [(STEPS + top_step(v), "top", (i + 2, v)) for v in range(CT * HEADS) if top_step(v) < 0]
            if i + 1 < CHUNKS:
                uses += [(top_step(v), "top", (i + 1, v)) for v in range(CT * HEADS) if top_step(v) >= 0]
                uses += [(15, "rows", i + 1)]
            if i > 0:
                uses += [(7, "finish", i - 1)]
            if i % CPG == 0 and i // CPG + 1 < GRAPHS:
                g = i // CPG + 1
                uses += [(9, "x_t", g), (12, "q_k", g)] + [(16 + 2 * a, "values", (g, a)) for a in range(CPG)]
            return sorted(uses, key=lambda u: u[0])

        def top_step(v):
            return v * STEPS // (CT * HEADS) - 10

        use_no = {}
        for i in range(-1, CHUNKS):
            for _, kind, arg in turn_uses(i):
                use_no[kind, arg] = len(use_no) + 1
        use_no["finish", CHUNKS - 1] = len(use_no) + 1

        class Place:

            def __init__(self, k, turn_reg=None):
                self.k, self.reg = k, turn_reg

            def count(self, of):
                if self.reg is None:
                    return of(self.k)
                first, per = of(self.k), of(self.k + LOOPED) - of(self.k)
                assert first > 0 and all(
                    of(self.k + LOOPED * (r + 1)) - of(self.k + LOOPED * r) == per for r in range(TURNS - 1))
                return self.reg * per + first

            def apart(self, eng):
                if self.reg is not None:
                    eng.nop(nofuse=True)

            def graph(self, g):
                if self.reg is None:
                    return g(self.k)
                return self.reg * 2 + g(self.k)

        def walk(eng, step):
            for u in range(CUT):
                step(Place(0), u)
            with eng.Fori(0, TURNS) as reg:
                for s in range(CUT, CUT + LOOPED * STEPS):
                    step(Place(s // STEPS, reg), s % STEPS)
            for s in range(CUT, LOOPED * STEPS):
                step(Place(TURNS * LOOPED + s // STEPS), s % STEPS)

        def maxima(g):
            return g - (g + SHARE - 2) // SHARE

        def par(k):
            return (k // CPG) % 2

        def use(kind, arg_of):
            return lambda i: use_no[kind, arg_of(i)]

        @block.sync
        def _(sp):
            sp.dma_start(x_in[:, :, :], x[0].rearrange("(t p) f -> p t f", p=TILE)).then_inc(x_landed, 16)
            sp.dma_start(w_scores[:, 0], w_self.rearrange("h f d -> f h d")).then_inc(weights_in, 16)
            sp.dma_start(w_scores[:, 1], w_other.rearrange("h f d -> f h d")).then_inc(weights_in, 16)
            sp.dma_start(w_values[:, :, :], w_value.rearrange("h f d -> f h d")).then_inc(weights_in, 16)
            sp.dma_start(bias_row[:, :], bias.rearrange("a b h d -> (a b) (h d)").to_broadcast([TILE, F])
                         ).then_inc(weights_in, 16)

            def load_adj(place, graph, chunk_of_graph, t):
                rows = chunk_of_graph * CHUNK + t * TILE
                sp.dma_start(adj_in[:, t, :], adj[graph, rows:rows + TILE, :]
                             ).then_inc(adj_landed[t], 16)

            def load_stacks(k):
                parts = (part1, part2, part3)
                order = ((0, 0), (0, 1), (0, 2), (1, 0), (1, 1), (2, 0))
                for h in range(HEADS):
                    for g, (pq, pk) in enumerate(order):
                        rows = slice(g * D, (g + 1) * D)
                        sp.dma_start(q_stack[rows, par(k), h, :], parts[pq][h * D:(h + 1) * D, :]
                                     ).then_inc(stacks_landed[h], 16)
                        sp.dma_start(k_stack[rows, par(k), h, :], parts[pk][64 + h * D:64 + (h + 1) * D, :]
                                     ).then_inc(stacks_landed[h], 16)

            def load_rows(k):
                c = k % CPG
                for h in range(HEADS):
                    sp.dma_start(q_stack[PARTS:ROWS, par(k), h, c * CHUNK:(c + 1) * CHUNK],
                                 shift_rows[3 * h:3 * h + 3, :]).then_inc(shifts_landed, 16)

            for t in range(CT):
                load_adj(None, 0, 0, t)
            sp.wait_ge(part3_ready, 1)
            load_stacks(0)
            for t in range(CT):
                sp.wait_ge(mask_ready, t + 1)
                load_adj(None, 0, 1, t)
            sp.wait_ge(turn_read, use_no["rows", 0])
            load_rows(0)

            def step(place, u):
                k, static = place.k, place.reg is None
                if u == 0:
                    if not static or k + 2 < CHUNKS:
                        for t in range(CT):
                            sp.wait_ge(mask_ready, place.count(lambda i: CT * (i + 1) + t + 1))
                            load_adj(place, place.graph(lambda i: (i + 2) // CPG), (k + 2) % CPG, t)
                    if k % CPG == 0 and (not static or k // CPG + 1 < GRAPHS):
                        sp.wait_ge(turn_full, place.count(use("x_t", lambda i: i // CPG)))
                        sp.dma_start(x_in[:, :, :],
                                     x[place.graph(lambda i: i // CPG + 1)].rearrange("(t p) f -> p t f", p=TILE)
                                     ).then_inc(x_landed, 16)
                if u == 1 and k % CPG == 1 and (not static or k // CPG + 1 < GRAPHS):
                    sp.wait_ge(part3_ready, place.count(lambda i: i // CPG + 2))
                    load_stacks(k + CPG)
                if u == 15 and not (static and k == 0):
                    store_chunk(place)
                if u == 15:
                    if not (static and k == 0):
                        sp.wait_ge(hidden_ready, place.count(lambda i: i))
                    rows = (k % CPG) * CHUNK
                    sp.dma_start(residual[:, :, :],
                                 x[place.graph(lambda i: i // CPG), rows:rows + CHUNK, :].rearrange(
                                     "(t p) f -> p t f", p=TILE)).then_inc(residual_landed, 16)
                if u == 17 and (not static or k + 1 < CHUNKS):
                    sp.wait_ge(turn_read, place.count(lambda i: use_no["rows", i + 1]))
                    load_rows(k + 1)

            def store_chunk(place):
                sp.wait_ge(normed_ready, place.count(lambda i: i))
                rows = ((place.k - 1) % CPG) * CHUNK
                sp.dma_start(out[place.graph(lambda i: (i - 1) // CPG), rows:rows + CHUNK, :].rearrange(
                    "(t p) f -> p t f", p=TILE), normed[:, :, :]).then_inc(out_landed, 16)
                sp.wait_ge(out_landed, place.count(lambda i: 16 * i))

            walk(sp, step)
            store_chunk(Place(CHUNKS))

        @block.gpsimd
        def _(gp):
            gp.memset(eye[:, :], 0.0).then_inc(consts_gp, 1)
            gp.memset(eye_pair[:, :, :], 0.0).then_inc(consts_gp, 1)
            gp.memset(minus_half[:, :], -0.5).then_inc(consts_gp, 1)
            gp.wait_ge(consts_gp, 3)
            gp.affine_select(out=eye[:, :], in_=eye[:, :], compare_op=ALU.not_equal, fill=1.0, base=0,
                             pattern=[[-1, 128]], channel_multiplier=1).then_inc(consts_gp, 1)
            gp.affine_select(out=eye_pair[:, :, :], in_=eye_pair[:, :, :], compare_op=ALU.not_equal, fill=1.0,
                             base=0, pattern=[[0, 2], [-1, TILE]], channel_multiplier=1).then_inc(consts_gp, 1)
            gp.wait_ge(consts_gp, 5)

            def make_mask(place, ahead, t):
                gp.wait_ge(adj_landed[t], place.count(lambda i: 16 * (i + ahead + 1)))
                place.apart(gp)
                gp.tensor_scalar(mask[:, (place.k + ahead) % CPG, t, :], adj_in[:, t, :], -1.0, MASKED,
                                 ALU.add, ALU.mult).then_inc(mask_ready, 1)

            def split(place, ahead):
                gp.wait_ge(turn_read, place.count(lambda i: use_no["q_k", i // CPG + ahead]))
                place.apart(gp)
                gp.tensor_scalar(part2[:, :], rest[:, :], 0.0, 1.0, ALU.add, ALU.mult).then_inc(part2_ready, 1)
                gp.wait_ge(part2_ready, place.count(lambda i: i // CPG + ahead + 1))
                place.apart(gp)
                gp.tensor_tensor(part3[:, :], rest[:, :], part2[:, :], ALU.subtract).then_inc(part3_ready, 1)

            def make_shift(place, ahead):
                def done(m):
                    gp.wait_ge(shift_step, place.count(lambda i: 5 * (i + ahead) + m))
                    place.apart(gp)
                gp.wait_ge(turn_read, place.count(lambda i: use_no["top", (i + ahead, CT * HEADS - 1)]))
                place.apart(gp)
                gp.tensor_scalar(clipped[:, :, :], top[:, (place.k + ahead) % 2], HIGH, LOW, ALU.min, ALU.max).then_inc(shift_step, 1)
                done(1)
                gp.tensor_tensor(minus_shift[:, :, :], clipped[:, :, :], top[:, (place.k + ahead) % 2],
                                 ALU.subtract).then_inc(shift_step, 1)
                done(2)
                gp.tensor_scalar(shift_parts[:, :, :, 0], minus_shift[:, :, :], 0.0, 1.0, ALU.add, ALU.mult).then_inc(shift_step, 1)
                done(3)
                gp.tensor_tensor(shift_rest[:, :, :], minus_shift[:, :, :], shift_parts[:, :, :, 0],
                                 ALU.subtract).then_inc(shift_step, 1)
                done(4)
                gp.tensor_scalar(shift_parts[:, :, :, 1], shift_rest[:, :, :], 0.0, 1.0, ALU.add, ALU.mult).then_inc(shift_step, 1)
                done(5)
                gp.tensor_tensor(shift_parts[:, :, :, 2], shift_rest[:, :, :], shift_parts[:, :, :, 1],
                                 ALU.subtract).then_inc(shift_ready, 1)

            def add_residual(place):
                def done(m):
                    gp.wait_ge(hidden_step, place.count(lambda i: 2 * (i - 1) + m))
                    place.apart(gp)
                gp.wait_ge(turn_read, place.count(lambda i: use_no["finish", i - 1]))
                place.apart(gp)
                gp.tensor_tensor(hidden[:, :, :], hidden[:, :, :],
                                 bias_row[:, :].rearrange("p (a f) -> p a f", a=1).to_broadcast([TILE, CT, F]),
                                 ALU.add).then_inc(hidden_step, 1)
                done(1)
                gp.tensor_scalar(hidden[:, :, :], hidden[:, :, :], 0.0, 1.0, ALU.max,
                                 ALU.mult).then_inc(hidden_step, 1)
                done(2)
                gp.wait_ge(residual_landed, place.count(lambda i: 16 * i))
                place.apart(gp)
                gp.tensor_tensor(hidden[:, :, :], hidden[:, :, :], residual[:, :, :],
                                 ALU.add).then_inc(hidden_ready, 1)

            def norm(place):
                gp.wait_ge(stats_ready, place.count(lambda i: i))
                place.apart(gp)
                gp.tensor_scalar(var_eps[:, :], moments[:, :, 1], EPS, 1.0, ALU.add, ALU.mult).then_inc(rstd_step, 1)
                gp.wait_ge(rstd_step, place.count(lambda i: 2 * (i - 1) + 1))
                place.apart(gp)
                gp.tensor_tensor(rstd[:, :], var_eps[:, :], minus_half[:, :], ALU.pow).then_inc(rstd_step, 1)
                gp.wait_ge(rstd_step, place.count(lambda i: 2 * (i - 1) + 2))
                place.apart(gp)
                for t in range(CT):
                    last = gp.tensor_scalar(normed[:, t, :], hidden[:, t, :], moments[:, t, 0:1], rstd[:, t:t + 1],
                                            ALU.subtract, ALU.mult)
                last.then_inc(normed_ready, 1)

            MASK_STEPS = (0, 2, 4, 6)

            def leaky_product(place, u):
                g = STEPS * place.k + u
                factor = factors[:, (g // SHARE) % COLDS].rearrange("p j h n -> p (j h n)")
                probs = exps[:, g % EXPS].rearrange("p j h n -> p (j h n)")
                gp.wait_ge(exps_done, place.count(lambda i: STEPS * i + u + 1))
                place.apart(gp)
                gp.tensor_scalar(factor, factor, 3e38, 1.0, ALU.min, ALU.max).then_inc(factor_ready, 1)
                gp.wait_ge(factor_ready, place.count(lambda i: (STEPS * i + u) // SHARE + 1))
                place.apart(gp)
                gp.tensor_tensor(probs, probs, factor, ALU.mult).then_inc(products_ready, 1)

            gp.wait_ge(weights_in, 64)
            split(Place(0), 0)
            for ahead in range(2):
                for t in range(CT):
                    make_mask(Place(0), ahead, t)
            make_shift(Place(0), 0)

            def step(place, u):
                k, static = place.k, place.reg is None
                if u in MASK_STEPS and (not static or k + 2 < CHUNKS):
                    if u == MASK_STEPS[0] and not (static and k == 0):
                        gp.wait_ge(scores_full, place.count(lambda i: STEPS * i))
                        place.apart(gp)
                    make_mask(place, 2, MASK_STEPS.index(u))
                if u == 8 and not (static and k == 0):
                    add_residual(place)
                if u == 12 and k % CPG == 0 and (not static or k // CPG + 1 < GRAPHS):
                    split(place, 1)
                if u == 14 and not (static and k == 0):
                    norm(place)
                if u == 13 and (not static or k + 1 < CHUNKS):
                    make_shift(place, 1)
                if u % SHARE == 1:
                    leaky_product(place, u)

            walk(gp, step)
            add_residual(Place(CHUNKS))
            gp.wait_ge(out_landed, 16 * (CHUNKS - 1))
            norm(Place(CHUNKS))

        @block.scalar
        def _(act):
            def use_turn(place, kind, arg_of, k, a):
                if kind not in ("x_t", "q_k", "values", "rows"):
                    return
                act.wait_ge(turn_full, place.count(use(kind, arg_of)))
                if kind == "x_t":
                    act.copy(x_t[:, :].rearrange("f (a n) -> f a n", a=CPG),
                             turn[0:F, :, 0:CHUNK]).then_inc(turn_read, 1)
                elif kind == "q_k":
                    act.copy(part1[:, :].rearrange("f (a n) -> f a n", a=CPG),
                             turn[:, :, 0:CHUNK]).then_inc(part1_ready, 1)
                elif kind == "values":
                    act.copy(values[:, par(k), a * CT:(a + 1) * CT, :, 0:D],
                             turn[0:TILE, a, 0:CT * F].rearrange("p (t h d) -> p t h d", t=CT, h=HEADS)
                             ).then_inc(turn_read, 1)
                elif kind == "rows":
                    act.copy(shift_rows[:, :], turn[0:3 * HEADS, 0, 0:CHUNK]).then_inc(turn_read, 1)

            def empty_attended(place):
                act.wait_ge(attended_done, place.count(lambda i: TILES * i))
                act.copy(sums[:, :], attended[:, 0:CHUNK]).then_inc(attended_free, 1)

            for _, kind, arg in turn_uses(-1):
                use_turn(Place(-1), kind, lambda i: arg, 0, arg[1] if kind == "values" else None)

            def step(place, u):
                k, static = place.k, place.reg is None
                g, half = STEPS * k + u, (STEPS * k + u) // 2
                act.wait_ge(scores_full, place.count(lambda i: STEPS * i + u + 1))
                if u % 2 == 0 and not (static and k == 0 and u < EXPS):
                    act.wait_ge(attended_done, place.count(lambda i: (STEPS * i + u) // 2 - EXPS // 2 + 1))
                both = [scores[:, g % 2, :, 0:CHUNK], exps[:, g % EXPS].rearrange("p j h n -> p j (h n)")]
                if u % SHARE == 1:
                    act.activation(both[1], both[0], ACT.Exp, scale=SCALE * SLOPE)
                    if not (static and k == 0 and u < COLDS * SHARE):
                        act.wait_ge(products_ready, place.count(lambda i: (STEPS * i + u) // SHARE - COLDS + 1))
                    act.activation(factors[:, (g // SHARE) % COLDS].rearrange("p j h n -> p j (h n)"), both[0],
                                   ACT.Exp, scale=SCALE * (1 - SLOPE)).then_inc(exps_done, 1)
                else:
                    act.activation(both[1], both[0], ACT.Exp, scale=SCALE)
                    if not (static and k == 0 and maxima(u) < COLDS):
                        act.wait_ge(probs_ready, place.count(lambda i: maxima(STEPS * i + u) - COLDS + 1))
                    act.activation(colds[:, maxima(g) % COLDS].rearrange("p j h n -> p j (h n)"), both[0],
                                   ACT.Exp, scale=SCALE * SLOPE).then_inc(exps_done, 1)
                if u == LAG - 1 and not (static and k == 0):
                    empty_attended(place)
                for s, kind, arg in turn_uses(k + (LOOPED if not static else 0)):
                    if s == u:
                        if kind == "rows":
                            use_turn(place, kind, lambda i: i + 1, k, None)
                        elif kind == "values":
                            use_turn(place, kind, lambda i: (i // CPG + 1, arg[1]), k + CPG, arg[1])
                        else:
                            use_turn(place, kind, lambda i: i // CPG + 1, k + CPG, None)

            walk(act, step)
            empty_attended(Place(CHUNKS))

        @block.vector
        def _(ve):
            ve.memset(values[:, :, :, :, :], 0.0).then_inc(consts_ve, 1)
            ve.wait_ge(consts_ve, 1)
            ve.memset(values[:, :, :, :, D:D + 1], 1.0).then_inc(consts_ve, 1)
            ve.memset(k_stack[PARTS:ROWS, :, :, :], 1.0).then_inc(consts_ve, 1)

            def top_of(place, ahead, v):
                t, h, chunk = v // HEADS, v % HEADS, place.k + ahead
                c = chunk % CPG
                if h == 0:
                    ve.wait_ge(mask_ready, place.count(lambda i: CT * (i + ahead) + t + 1))
                if v == 0 and not (place.reg is None and chunk < 2):
                    ve.wait_ge(shift_ready, place.count(lambda i: i + ahead - 1))
                ve.wait_ge(turn_full, place.count(lambda i: use_no["top", (i + ahead, v)]))
                place.apart(ve)
                ve.tensor_tensor_reduce(
                    out=masked_out[:, :].rearrange("p (a m) -> p a m", a=CPG), in0=turn[0:TILE, :, 0:CHUNK],
                    in1=mask[:, c, t, :].rearrange("p (a m) -> p a m", a=CPG), scale=1.0, scalar=LOWEST,
                    op0=ALU.add, op1=ALU.max, accum_out=top[:, chunk % 2, t, h:h + 1]).then_inc(turn_read, 1)

            def rest_of(place, g_of):
                ve.wait_ge(part1_ready, place.count(lambda i: g_of(i) + 1))
                ve.tensor_tensor(rest[:, :].rearrange("f (a n) -> f a n", a=CPG), turn[:, :, 0:CHUNK],
                                 part1[:, :].rearrange("f (a n) -> f a n", a=CPG),
                                 ALU.subtract).then_inc(turn_read, 1)

            def finish(place):
                ve.wait_ge(turn_full, place.count(lambda i: use_no["finish", i - 1]))
                both = turn[0:TILE, 0, :].rearrange("p (t h d) -> p t h d", t=CT, h=HEADS)
                ve.tensor_scalar(floor_z[:, :, :], both[:, :, :, D], 1e-30, None, ALU.max).then_inc(norm_z, 1)
                ve.wait_ge(norm_z, place.count(lambda i: 2 * (i - 1) + 1))
                ve.reciprocal(recip_z[:, :, :], floor_z[:, :, :]).then_inc(norm_z, 1)
                ve.wait_ge(norm_z, place.count(lambda i: 2 * (i - 1) + 2))
                ve.tensor_tensor(hidden[:, :, :].rearrange("p t (h d) -> p (t h) d", h=HEADS),
                                 turn[0:TILE, 0, :].rearrange("p (t d) -> p t d", d=32)[:, :, 0:D],
                                 recip_z[:, :, :].rearrange("p t (h a) -> p (t h) a", a=1).to_broadcast(
                                     [TILE, CT * HEADS, D]),
                                 ALU.mult).then_inc(turn_read, 1)

            def statistics(place):
                ve.wait_ge(hidden_ready, place.count(lambda i: i))
                for t in range(CT):
                    last = ve.bn_stats(stats[:, t, :], hidden[:, t, :])
                last.then_inc(stats_step, 1)
                ve.wait_ge(stats_step, place.count(lambda i: i))
                place.apart(ve)
                for t in range(CT):
                    last = ve.bn_aggr(moments[:, t, :], stats[:, t, :])
                last.then_inc(stats_ready, 1)

            rest_of(Place(0), lambda i: 0)
            for _, kind, arg in turn_uses(-1):
                if kind == "top":
                    top_of(Place(0), arg[0], arg[1])

            def step(place, u):
                k, static = place.k, place.reg is None
                for s, kind, arg in turn_uses(k + (LOOPED if not static else 0)):
                    if s == u and kind == "top":
                        top_of(place, 1 if top_step(arg[1]) >= 0 else 2, arg[1])
                    elif s == u and kind == "q_k":
                        rest_of(place, lambda i: i // CPG + 1)
                    elif s == u and kind == "finish":
                        finish(place)
                if u == 13 and not (static and k == 0):
                    statistics(place)
                if u % SHARE != 1:
                    g = STEPS * k + u
                    ve.wait_ge(exps_done, place.count(lambda i: STEPS * i + u + 1))
                    ve.tensor_tensor(exps[:, g % EXPS].rearrange("p j h n -> p (j h n)"),
                                     exps[:, g % EXPS].rearrange("p j h n -> p (j h n)"),
                                     colds[:, maxima(g) % COLDS].rearrange("p j h n -> p (j h n)"),
                                     ALU.max).then_inc(probs_ready, 1)

            walk(ve, step)
            ve.wait_ge(normed_ready, CHUNKS - 1)
            finish(Place(CHUNKS))
            statistics(Place(CHUNKS))

        @block.tensor
        def _(pe):
            def product_in_turn(place, kind, arg_of, no_of, v, k):
                if not (place.reg is None and no_of(place.k) == 1):
                    pe.wait_ge(turn_read, place.count(lambda i: no_of(i) - 1))
                if kind == "x_t":
                    pe.wait_ge(x_landed, place.count(lambda i: 16 * (arg_of(i) + 1)))
                    place.apart(pe)
                    for t in range(TILES):
                        last = pe.transpose(turn[0:F, t // CT, (t % CT) * TILE:(t % CT + 1) * TILE],
                                            x_in[:, t, :], eye[0:TILE, 0:TILE])
                elif kind == "q_k":
                    pe.wait_ge(turn_read, place.count(lambda i: use_no["x_t", arg_of(i)]))
                    for a in range(CPG):
                        last = pe.matmul(turn[:, a, 0:CHUNK], w_scores[:, :, :, :].rearrange("f a h d -> f (a h d)"),
                                         x_t[:, a * CHUNK:(a + 1) * CHUNK], start=True, stop=True)
                elif kind == "values":
                    for t in range(v * CT, (v + 1) * CT):
                        last = pe.matmul(turn[0:TILE, t // CT, (t % CT) * F:(t % CT + 1) * F],
                                         x_t[:, t * TILE:(t + 1) * TILE],
                                         w_values[:, :, :].rearrange("f h d -> f (h d)"), start=True, stop=True)
                elif kind == "top":
                    t, h = v // HEADS, v % HEADS
                    if t == 0:
                        pe.wait_ge(stacks_landed[h], place.count(lambda i: 16 * 12 * (arg_of(i) // CPG + 1)))
                    n0 = (k % CPG) * CHUNK + t * TILE
                    for a in range(CPG):
                        last = pe.matmul(turn[0:TILE, a, 0:CHUNK], q_stack[0:PARTS, par(k), h, n0:n0 + TILE],
                                         k_stack[0:PARTS, par(k), h, a * CHUNK:(a + 1) * CHUNK],
                                         start=True, stop=True)
                elif kind == "rows":
                    pe.wait_ge(shift_ready, place.count(lambda i: arg_of(i) + 1))
                    for t in range(CT):
                        last = pe.matmul(turn[0:3 * HEADS, 0, t * TILE:(t + 1) * TILE],
                                         shift_parts[:, t, :, :].rearrange("p h l -> p (h l)"),
                                         eye_pair[:, 0, :], start=True, stop=True)
                elif kind == "finish":
                    pe.wait_ge(attended_free, place.count(lambda i: arg_of(i) + 1))
                    place.apart(pe)
                    for t in range(CT):
                        last = pe.transpose(turn[0:TILE, 0, t * 128:(t + 1) * 128], sums[:, t * TILE:(t + 1) * TILE],
                                            eye[:, :])
                last.then_inc(turn_full, 1)

            def attend(place, mt):
                k = place.k
                pe.wait_ge(probs_ready, place.count(lambda i: maxima(STEPS * i + 2 * mt + 2)))
                if (2 * mt + 1) % SHARE == 1:
                    pe.wait_ge(products_ready, place.count(lambda i: (STEPS * i + 2 * mt + 1) // SHARE + 1))
                if mt == 0 and not (place.reg is None and k == 0):
                    pe.wait_ge(attended_free, place.count(lambda i: i))
                for h in range(HEADS):
                    g = STEPS * k + 2 * mt + h // 2
                    last = pe.matmul(attended[32 * h:32 * h + 32, 0:CHUNK], values[:, par(k), mt, h, :],
                                     exps[:, g % EXPS, :, h % 2, :], start=mt == 0, stop=mt == TILES - 1,
                                     skip_group_check=True)
                last.then_inc(attended_done, 1)

            pe.wait_ge(weights_in, 64)
            pe.wait_ge(consts_gp, 5)
            pe.wait_ge(consts_ve, 3)
            for _, kind, arg in turn_uses(-1):
                chunk, v = arg if kind in ("top", "values") else (arg, None)
                product_in_turn(Place(0), kind, lambda i: chunk, use(kind, lambda i: arg), v, chunk)

            def step(place, u):
                k, static = place.k, place.reg is None
                g, mt, pair = STEPS * k + u, u // 2, u % 2
                c, p = k % CPG, par(k)
                if u == 0:
                    pe.wait_ge(mask_ready, place.count(lambda i: CT * (i + 1)))
                    pe.wait_ge(shifts_landed, place.count(lambda i: 16 * HEADS * (i + 1)))
                if not (static and k == 0 and u < 2):
                    pe.wait_ge(exps_done, place.count(lambda i: STEPS * i + u - 1))
                m = slice(mt * TILE, (mt + 1) * TILE)
                for j in range(2):
                    for s in range(2):
                        pe.matmul(scores[:, g % 2, j, 0:CHUNK].rearrange("m (h n) -> m h n", h=2)[
                                      :, :, s * TILE:(s + 1) * TILE],
                                  mask[:, c, 2 * j + s, m], eye_pair[:, :, :], start=s == 0, stop=False,
                                  skip_group_check=True)
                    for hp in range(2):
                        h, n0 = 2 * pair + hp, c * CHUNK + j * HALF
                        last = pe.matmul(scores[:, g % 2, j, hp * HALF:(hp + 1) * HALF], k_stack[:, p, h, m],
                                         q_stack[:, p, h, n0:n0 + HALF], start=False, stop=True,
                                         skip_group_check=True)
                last.then_inc(scores_full, 1)
                if u % 2 == 0:
                    if u >= LAG:
                        attend(place, mt - LAG // 2)
                    elif not (static and k == 0):
                        attend(Place(k - 1, place.reg), TILES + mt - LAG // 2)
                for s, kind, arg in turn_uses(k + (LOOPED if not static else 0)):
                    if s != u:
                        continue
                    if kind == "top":
                        v = arg[1]
                        ahead = 1 if top_step(v) >= 0 else 2
                        product_in_turn(place, kind, lambda i: i + ahead, lambda i: use_no["top", (i + ahead, v)], v,
                                        k + ahead)
                    elif kind == "rows":
                        product_in_turn(place, kind, lambda i: i + 1, lambda i: use_no["rows", i + 1], None, k + 1)
                    elif kind == "finish":
                        product_in_turn(place, kind, lambda i: i - 1, lambda i: use_no["finish", i - 1], None, k)
                    elif kind == "values":
                        product_in_turn(place, kind, lambda i: i // CPG + 1,
                                        lambda i: use_no["values", (i // CPG + 1, arg[1])], arg[1], k + CPG)
                    else:
                        product_in_turn(place, kind, lambda i: i // CPG + 1,
                                        lambda i, kind=kind: use_no[kind, i // CPG + 1], None, k + CPG)

            walk(pe, step)
            for mt in range(TILES - LAG // 2, TILES):
                attend(Place(CHUNKS - 1), mt)
            product_in_turn(Place(CHUNKS), "finish", lambda i: i - 1, lambda i: use_no["finish", i - 1], None, CHUNKS)


_INS = ['x', 'adj', 'L0_gnn_kernel', 'L0_gnn_attention_kernel', 'L0_gnn_attention_kernel_2', 'L0_gnn_bias']


def kernel(**inputs):
    import numpy as _np
    import concourse.bacc as _bacc
    from concourse import mybir as _mybir
    from concourse.bass_utils import run_bass_kernel_spmd as _run

    nc = _bacc.Bacc("TRN2", target_bir_lowering=False, num_devices=1)
    arrays, args = {}, []
    for name in _INS:
        a = _np.ascontiguousarray(inputs[name])
        arrays[f"in_{name}_dram"] = a
        args.append(nc.dram_tensor(f"in_{name}_dram", a.shape, _mybir.dt.from_np(a.dtype), kind="ExternalInput").ap())
    shape = tuple(inputs['x'].shape)
    args.append(nc.dram_tensor("out_0_dram", shape, _mybir.dt.float32, kind="ExternalOutput").ap())
    graph_attention_resnorm(nc, *args)
    r = _run(nc, [arrays], core_ids=[0])
    return r.results[0]["out_0_dram"]
```

```python
import concourse.bass as bass
from concourse import mybir
from contextlib import ExitStack


def graph_attention_resnorm(nc: bass.Bass, x: bass.AP, adj: bass.AP, w_value: bass.AP, w_self: bass.AP,
                            w_other: bass.AP, bias: bass.AP, out: bass.AP):
    F32, BF16 = mybir.dt.float32, mybir.dt.bfloat16
    ALU, ACT = mybir.AluOpType, mybir.ActivationFunctionType

    GRAPHS, N, F = x.shape
    HEADS, _, D = w_value.shape
    TILE = 125
    TILES = N // TILE
    CT = 4
    CHUNK = CT * TILE
    CPG = TILES // CT
    CHUNKS = GRAPHS * CPG
    HALF = CHUNK // 2
    STEPS = TILES * 2
    PARTS = 6 * D
    ROWS = PARTS + 3 * HEADS
    MASKED = 1e30
    LOWEST = -1e12
    LOW, HIGH = -400.0, 160.0
    SLOPE, SCALE, EPS = 0.2, D ** -0.5, 1e-5
    EXPS, COLDS = 8, 2
    GP_STEPS = (1, 5, 9, 13, 16, 19, 22)
    LAG = 6
    LOOPED = 2 * CPG
    CUT = 16
    TURNS = CHUNKS // LOOPED - 1

    ctx = ExitStack()
    with ctx:
        def sb(name, shape, dt=F32):
            return ctx.enter_context(nc.sbuf_tensor(name, shape, dt))

        def sem(name):
            return ctx.enter_context(nc.semaphore(name))

        eye = sb("eye", [128, 128])
        eye_pair = sb("eye_pair", [TILE, 2, TILE], BF16)
        w_scores = sb("w_scores", [2 * F, 2, HEADS, D])
        w_values = sb("w_values", [2 * F, HEADS, D])
        bias_row = sb("bias_row", [TILE, F])
        own_head = sb("own_head", [128, HEADS], BF16)
        minus_half = sb("minus_half", [TILE, CT])
        adj_in = sb("adj_in", [TILE, CT, N])
        x_in = sb("x_in", [TILE, TILES, F])
        residual = sb("residual", [TILE, CT, F])
        mask = sb("mask", [TILE, CPG, CT, N], BF16)
        q_stack = sb("q_stack", [ROWS, 2, HEADS, N], BF16)
        k_stack = sb("k_stack", [ROWS, 2, HEADS, N], BF16)
        values = sb("values", [TILE, 2, TILES, HEADS, 32])
        x_t = sb("x_t", [2 * F, TILES // 2, TILE])
        part1 = sb("part1", [128, N], BF16)
        part2 = sb("part2", [128, N], BF16)
        part3 = sb("part3", [128, N], BF16)
        rest = sb("rest", [128, N])
        masked_out = sb("masked_out", [TILE, 2, N], BF16)
        top = sb("top", [TILE, 2, CT, HEADS])
        clipped = sb("clipped", [TILE, CT, HEADS])
        minus_shift = sb("minus_shift", [TILE, CT, HEADS])
        shift_rest = sb("shift_rest", [TILE, CT, HEADS])
        shift_parts = sb("shift_parts", [128, CT, 32], BF16)
        shift_blocks = sb("shift_blocks", [128, CT, 32], BF16)
        exps = sb("exps", [TILE, EXPS, 2, 2, HALF])
        colds = sb("colds", [TILE, COLDS, 2, 2, HALF])
        factors = sb("factors", [TILE, COLDS, 2, 2, HALF])
        sums = sb("sums", [128, CHUNK])
        floor_z = sb("floor_z", [TILE, CT, HEADS])
        recip_z = sb("recip_z", [TILE, CT, HEADS])
        hidden = sb("hidden", [TILE, CT, F])
        stats = sb("stats", [TILE, CT, 6])
        moments = sb("moments", [TILE, CT, 2])
        var_eps = sb("var_eps", [TILE, CT])
        rstd = sb("rstd", [TILE, CT])
        normed = sb("normed", [TILE, CT, F])

        scores = ctx.enter_context(nc.psum_tensor("scores", [TILE, 2, 2, 512], F32))
        turn = ctx.enter_context(nc.psum_tensor("turn", [128, 3, 512], F32))
        attended = ctx.enter_context(nc.psum_tensor("attended", [128, 512], F32))

        scores_banks = scores[:, :, :, :].rearrange("m s j n -> m (s j) n")

        weights_in = sem("weights_in")
        x_landed = sem("x_landed")
        adj_landed = [sem(f"adj_landed{t}") for t in range(CT)]
        residual_landed = sem("residual_landed")
        stacks_landed = [sem(f"stacks_landed{h}") for h in range(HEADS)]
        shifts_landed = sem("shifts_landed")
        out_landed = sem("out_landed")
        consts_gp = sem("consts_gp")
        consts_ve = sem("consts_ve")
        turn_full = sem("turn_full")
        turn_read = sem("turn_read")
        mask_ready = sem("mask_ready")
        part1_ready = sem("part1_ready")
        part2_ready = sem("part2_ready")
        part3_ready = sem("part3_ready")
        shift_step = sem("shift_step")
        shift_ready = sem("shift_ready")
        blocks_ready = sem("blocks_ready")
        scores_full = sem("scores_full")
        exps_done = sem("exps_done")
        probs_ready = sem("probs_ready")
        factor_ready = sem("factor_ready")
        products_ready = sem("products_ready")
        attended_done = sem("attended_done")
        attended_free = sem("attended_free")
        norm_z = sem("norm_z")
        hidden_step = sem("hidden_step")
        hidden_ready = sem("hidden_ready")
        stats_step = sem("stats_step")
        stats_ready = sem("stats_ready")
        rstd_step = sem("rstd_step")
        normed_ready = sem("normed_ready")

        VALUES_AT = [(1, 4), (1, 10)]
        VALUE_PAIRS = TILES // 2 // len(VALUES_AT)
        PAIRS = TILES // 4
        pairs_in_turn = turn[:, 0:2, 0:PAIRS * TILE].rearrange("p b (q n) -> p b q n", n=TILE)

        def in_pairs(of, a):
            return of[:, a * N // 2:(a + 1) * N // 2].rearrange("p (q b n) -> p b q n", q=PAIRS, b=2)

        block = ctx.enter_context(nc.Block())

        def turn_uses(i):
            if i < 0:
                return ([(0, "x_t", 0), (0, "q_k", (0, 0)), (0, "q_k", (0, 1))]
                        + [(0, "values", (0, piece)) for piece in range(len(VALUES_AT))]
                        + [(0, "top", (0, t * HEADS + h)) for h in range(HEADS) for t in range(CT)]
                        + [(0, "top", (1, v)) for v in range(CT * HEADS) if top_step(v) < 0])
            uses = []
            if i + 2 < CHUNKS:
                uses += [(STEPS + top_step(v), "top", (i + 2, v)) for v in range(CT * HEADS) if top_step(v) < 0]
            if i + 1 < CHUNKS:
                uses += [(top_step(v), "top", (i + 1, v)) for v in range(CT * HEADS) if top_step(v) >= 0]
            if i > 0:
                uses += [(7, "finish", i - 1)]
            if i % CPG == 0 and i // CPG + 1 < GRAPHS:
                g = i // CPG + 1
                uses += [(10, "x_t", g), (13, "q_k", (g, 0)), (16, "q_k", (g, 1))]
            if i // CPG + 1 < GRAPHS:
                uses += [(u, "values", (i // CPG + 1, piece)) for piece, (c, u) in enumerate(VALUES_AT)
                         if c == i % CPG]
            return sorted(uses, key=lambda u: u[0])

        def top_step(v):
            return v * STEPS // (CT * HEADS) - 10

        use_no = {}
        for i in range(-1, CHUNKS):
            for _, kind, arg in turn_uses(i):
                use_no[kind, arg] = len(use_no) + 1
        use_no["finish", CHUNKS - 1] = len(use_no) + 1

        early_tops = [arg for _, kind, arg in turn_uses(-1) if kind == "top"]

        def in_scores(arg):
            return arg in early_tops and early_tops.index(arg) % 2 == 1

        class Place:

            def __init__(self, k, turn_reg=None):
                self.k, self.reg = k, turn_reg

            def count(self, of):
                if self.reg is None:
                    return of(self.k)
                first, per = of(self.k), of(self.k + LOOPED) - of(self.k)
                assert first > 0 and all(
                    of(self.k + LOOPED * (r + 1)) - of(self.k + LOOPED * r) == per for r in range(TURNS - 1))
                return self.reg * per + first

            def apart(self, eng):
                if self.reg is not None:
                    eng.nop(nofuse=True)

            def graph(self, g):
                if self.reg is None:
                    return g(self.k)
                return self.reg * 2 + g(self.k)

        def walk(eng, step):
            for u in range(CUT):
                step(Place(0), u)
            with eng.Fori(0, TURNS) as reg:
                for s in range(CUT, CUT + LOOPED * STEPS):
                    step(Place(s // STEPS, reg), s % STEPS)
            for s in range(CUT, LOOPED * STEPS):
                step(Place(TURNS * LOOPED + s // STEPS), s % STEPS)

        def products(g):
            return g // STEPS * len(GP_STEPS) + sum(u < g % STEPS for u in GP_STEPS)

        def maxima(g):
            return g - products(g)

        def par(k):
            return (k // CPG) % 2

        def use(kind, arg_of):
            return lambda i: use_no[kind, arg_of(i)]

        @block.sync
        def _(sp):
            sp.dma_start(x_in[:, :, :], x[0].rearrange("(t p) f -> p t f", p=TILE)).then_inc(x_landed, 16)
            for half in (slice(0, F), slice(F, 2 * F)):
                sp.dma_start(w_scores[half, 0], w_self.rearrange("h f d -> f h d")).then_inc(weights_in, 16)
                sp.dma_start(w_scores[half, 1], w_other.rearrange("h f d -> f h d")).then_inc(weights_in, 16)
                sp.dma_start(w_values[half], w_value.rearrange("h f d -> f h d")).then_inc(weights_in, 16)
            sp.dma_start(bias_row[:, :], bias.rearrange("a b h d -> (a b) (h d)").to_broadcast([TILE, F])
                         ).then_inc(weights_in, 16)

            def load_adj(graph, chunk_of_graph, t):
                rows = chunk_of_graph * CHUNK + t * TILE
                sp.dma_start(adj_in[:, t, :], adj[graph, rows:rows + TILE, :]
                             ).then_inc(adj_landed[t], 16)

            def load_stacks(k, first=False):
                parts = (part1, part2, part3)
                order = ((0, 0), (0, 1), (0, 2), (1, 0), (1, 1), (2, 0))
                for h in range(HEADS):
                    for g, (pq, pk) in enumerate(order):
                        if first and h == 0 and g in (1, 2):
                            sp.wait_ge((part2_ready, part3_ready)[g - 1], 1)
                        rows = slice(g * D, (g + 1) * D)
                        sp.dma_start(q_stack[rows, par(k), h, :], parts[pq][h * D:(h + 1) * D, :]
                                     ).then_inc(stacks_landed[h], 16)
                        sp.dma_start(k_stack[rows, par(k), h, :], parts[pk][64 + h * D:64 + (h + 1) * D, :]
                                     ).then_inc(stacks_landed[h], 16)

            def load_shifts(k):
                c = k % CPG
                for b in range(4):
                    n = min(32, TILE - 32 * b)
                    src = shift_blocks[32 * b:32 * b + 3 * HEADS, :, 0:n]
                    for h in range(HEADS):
                        dst = q_stack[PARTS:ROWS, par(k), h, c * CHUNK:(c + 1) * CHUNK].rearrange(
                            "r (t n) -> r t n", t=CT)[:, :, 32 * b:32 * b + n]
                        sp.dma_start(dst, src).then_inc(shifts_landed, 16)

            for t in range(CT):
                load_adj(0, 0, t)
            sp.wait_ge(turn_read, use_no["q_k", (0, 1)])
            load_stacks(0, first=True)
            for t in range(CT):
                sp.wait_ge(mask_ready, t + 1)
                load_adj(0, 1, t)
            sp.wait_ge(blocks_ready, 1)
            load_shifts(0)

            def step(place, u):
                k, static = place.k, place.reg is None
                if u == 0:
                    if not static or k + 2 < CHUNKS:
                        for t in range(CT):
                            sp.wait_ge(mask_ready, place.count(lambda i: CT * (i + 1) + t + 1))
                            load_adj(place.graph(lambda i: (i + 2) // CPG), (k + 2) % CPG, t)
                    if k % CPG == 0 and (not static or k // CPG + 1 < GRAPHS):
                        sp.wait_ge(turn_full, place.count(use("x_t", lambda i: i // CPG)))
                        sp.dma_start(x_in[:, :, :],
                                     x[place.graph(lambda i: i // CPG + 1)].rearrange("(t p) f -> p t f", p=TILE)
                                     ).then_inc(x_landed, 16)
                if u == 1 and k % CPG == 1 and (not static or k // CPG + 1 < GRAPHS):
                    sp.wait_ge(part3_ready, place.count(lambda i: i // CPG + 2))
                    load_stacks(k + CPG)
                if u == 15 and (not static or k + 1 < CHUNKS):
                    sp.wait_ge(blocks_ready, place.count(lambda i: i + 2))
                    load_shifts(k + 1)
                if u == 15 and not (static and k == 0):
                    store_chunk(place)
                if u == 15:
                    if not (static and k == 0):
                        sp.wait_ge(hidden_ready, place.count(lambda i: i))
                    rows = (k % CPG) * CHUNK
                    sp.dma_start(residual[:, :, :],
                                 x[place.graph(lambda i: i // CPG), rows:rows + CHUNK, :].rearrange(
                                     "(t p) f -> p t f", p=TILE)).then_inc(residual_landed, 16)

            def store_chunk(place):
                sp.wait_ge(normed_ready, place.count(lambda i: i))
                rows = ((place.k - 1) % CPG) * CHUNK
                sp.dma_start(out[place.graph(lambda i: (i - 1) // CPG), rows:rows + CHUNK, :].rearrange(
                    "(t p) f -> p t f", p=TILE), normed[:, :, :]).then_inc(out_landed, 16)
                sp.wait_ge(out_landed, place.count(lambda i: 16 * i))

            walk(sp, step)
            store_chunk(Place(CHUNKS))

        @block.gpsimd
        def _(gp):
            gp.memset(eye[:, :], 0.0).then_inc(consts_gp, 1)
            gp.memset(eye_pair[:, :, :], 0.0).then_inc(consts_gp, 1)
            gp.memset(minus_half[:, :], -0.5).then_inc(consts_gp, 1)
            gp.memset(own_head[:, :], 1.0).then_inc(consts_gp, 1)
            gp.wait_ge(consts_gp, 4)
            gp.affine_select(out=eye[:, :], in_=eye[:, :], compare_op=ALU.not_equal, fill=1.0, base=0,
                             pattern=[[-1, 128]], channel_multiplier=1).then_inc(consts_gp, 1)
            gp.affine_select(out=eye_pair[:, :, :], in_=eye_pair[:, :, :], compare_op=ALU.not_equal, fill=1.0,
                             base=0, pattern=[[0, 2], [-1, TILE]], channel_multiplier=1).then_inc(consts_gp, 1)
            gp.affine_select(out=own_head[:, :], in_=own_head[:, :], compare_op=ALU.is_ge, fill=0.0, base=-PARTS,
                             pattern=[[-3, HEADS]], channel_multiplier=1).then_inc(consts_gp, 1)
            gp.wait_ge(consts_gp, 7)
            gp.affine_select(out=own_head[:, :], in_=own_head[:, :], compare_op=ALU.is_ge, fill=0.0, base=PARTS + 2,
                             pattern=[[3, HEADS]], channel_multiplier=-1).then_inc(consts_gp, 1)
            gp.wait_ge(consts_gp, 8)
            gp.wait_ge(weights_in, 16 * 7)

            def make_mask(place, ahead, t):
                gp.wait_ge(adj_landed[t], place.count(lambda i: 16 * (i + ahead + 1)))
                place.apart(gp)
                gp.tensor_scalar(mask[:, (place.k + ahead) % CPG, t, :], adj_in[:, t, :], -1.0, MASKED,
                                 ALU.add, ALU.mult).then_inc(mask_ready, 1)

            def split(place, ahead):
                gp.wait_ge(turn_read, place.count(lambda i: use_no["q_k", (i // CPG + ahead, 1)]))
                place.apart(gp)
                gp.tensor_scalar(part2[:, :], rest[:, :], 0.0, 1.0, ALU.add, ALU.mult).then_inc(part2_ready, 1)
                gp.wait_ge(part2_ready, place.count(lambda i: i // CPG + ahead + 1))
                place.apart(gp)
                gp.tensor_tensor(part3[:, :], rest[:, :], part2[:, :], ALU.subtract).then_inc(part3_ready, 1)

            def make_shift(place, ahead):
                def done(m):
                    gp.wait_ge(shift_step, place.count(lambda i: 5 * (i + ahead) + m))
                    place.apart(gp)
                def parts(m):
                    return shift_parts[0:TILE, :, 0:3 * HEADS].rearrange("p t (h m) -> p t h m", m=3)[:, :, :, m]
                gp.wait_ge(turn_read, place.count(lambda i: use_no["top", (i + ahead, CT * HEADS - 1)]))
                place.apart(gp)
                gp.tensor_scalar(clipped[:, :, :], top[:, (place.k + ahead) % 2], HIGH, LOW,
                                 ALU.min, ALU.max).then_inc(shift_step, 1)
                done(1)
                gp.tensor_tensor(minus_shift[:, :, :], clipped[:, :, :], top[:, (place.k + ahead) % 2],
                                 ALU.subtract).then_inc(shift_step, 1)
                done(2)
                gp.tensor_scalar(parts(0), minus_shift[:, :, :], 0.0, 1.0, ALU.add, ALU.mult).then_inc(shift_step, 1)
                done(3)
                gp.tensor_tensor(shift_rest[:, :, :], minus_shift[:, :, :], parts(0),
                                 ALU.subtract).then_inc(shift_step, 1)
                done(4)
                gp.tensor_scalar(parts(1), shift_rest[:, :, :], 0.0, 1.0, ALU.add, ALU.mult).then_inc(shift_step, 1)
                done(5)
                gp.tensor_tensor(parts(2), shift_rest[:, :, :], parts(1),
                                 ALU.subtract).then_inc(shift_ready, 1)

            def add_residual(place):
                def done(m):
                    gp.wait_ge(hidden_step, place.count(lambda i: 2 * (i - 1) + m))
                    place.apart(gp)
                gp.wait_ge(turn_read, place.count(lambda i: use_no["finish", i - 1]))
                place.apart(gp)
                gp.tensor_tensor(hidden[:, :, :], hidden[:, :, :],
                                 bias_row[:, :].rearrange("p (a f) -> p a f", a=1).to_broadcast([TILE, CT, F]),
                                 ALU.add).then_inc(hidden_step, 1)
                done(1)
                gp.tensor_scalar(hidden[:, :, :], hidden[:, :, :], 0.0, 1.0, ALU.max,
                                 ALU.mult).then_inc(hidden_step, 1)
                done(2)
                gp.wait_ge(residual_landed, place.count(lambda i: 16 * i))
                place.apart(gp)
                gp.tensor_tensor(hidden[:, :, :], hidden[:, :, :], residual[:, :, :],
                                 ALU.add).then_inc(hidden_ready, 1)

            def norm(place):
                gp.wait_ge(stats_ready, place.count(lambda i: i))
                place.apart(gp)
                gp.tensor_scalar(var_eps[:, :], moments[:, :, 1], EPS, 1.0, ALU.add, ALU.mult).then_inc(rstd_step, 1)
                gp.wait_ge(rstd_step, place.count(lambda i: 2 * (i - 1) + 1))
                place.apart(gp)
                gp.tensor_tensor(rstd[:, :], var_eps[:, :], minus_half[:, :], ALU.pow).then_inc(rstd_step, 1)
                gp.wait_ge(rstd_step, place.count(lambda i: 2 * (i - 1) + 2))
                place.apart(gp)
                for t in range(CT):
                    last = gp.tensor_scalar(normed[:, t, :], hidden[:, t, :], moments[:, t, 0:1], rstd[:, t:t + 1],
                                            ALU.subtract, ALU.mult)
                last.then_inc(normed_ready, 1)

            MASK_STEPS = (0, 2, 4, 6)

            def leaky_product(place, u):
                g = STEPS * place.k + u
                factor = factors[:, products(g) % COLDS].rearrange("p j h n -> p (j h n)")
                probs = exps[:, g % EXPS].rearrange("p j h n -> p (j h n)")
                gp.wait_ge(exps_done, place.count(lambda i: STEPS * i + u + 1))
                place.apart(gp)
                gp.tensor_scalar(factor, factor, 1.0, None, ALU.max).then_inc(factor_ready, 1)
                gp.wait_ge(factor_ready, place.count(lambda i: products(STEPS * i + u) + 1))
                place.apart(gp)
                gp.tensor_tensor(probs, probs, factor, ALU.mult).then_inc(products_ready, 1)

            split(Place(0), 0)
            for ahead in range(2):
                for t in range(CT):
                    make_mask(Place(0), ahead, t)
            make_shift(Place(0), 0)

            def step(place, u):
                k, static = place.k, place.reg is None
                if u in MASK_STEPS and (not static or k + 2 < CHUNKS):
                    if u == MASK_STEPS[0] and not (static and k == 0):
                        gp.wait_ge(scores_full, place.count(lambda i: STEPS * i))
                        place.apart(gp)
                    make_mask(place, 2, MASK_STEPS.index(u))
                if u == 8 and not (static and k == 0):
                    add_residual(place)
                if u == 15 and k % CPG == 0 and (not static or k // CPG + 1 < GRAPHS):
                    split(place, 1)
                if u == 14 and not (static and k == 0):
                    norm(place)
                if u == 13 and (not static or k + 1 < CHUNKS):
                    make_shift(place, 1)
                if u in GP_STEPS:
                    leaky_product(place, u)

            walk(gp, step)
            add_residual(Place(CHUNKS))
            gp.wait_ge(out_landed, 16 * (CHUNKS - 1))
            norm(Place(CHUNKS))

        @block.scalar
        def _(act):
            def use_turn(place, kind, arg_of, k, a):
                if kind not in ("x_t", "q_k", "values"):
                    return
                act.wait_ge(turn_full, place.count(use(kind, arg_of)))
                if kind == "x_t":
                    act.copy(x_t[:, :, :].rearrange("f (b q) n -> f b (q n)", b=2),
                             turn[:, 0:2, 0:PAIRS * TILE]).then_inc(turn_read, 1)
                elif kind == "q_k":
                    act.copy(in_pairs(part1, a), pairs_in_turn).then_inc(part1_ready, 1)
                elif kind == "values":
                    for odd in range(2):
                        last = act.copy(values[:, par(k), 2 * a * VALUE_PAIRS + odd:2 * (a + 1) * VALUE_PAIRS:2, :, 0:D],
                                        turn[0:TILE, odd, 0:VALUE_PAIRS * F].rearrange(
                                            "p (q h d) -> p q h d", q=VALUE_PAIRS, h=HEADS))
                    last.then_inc(turn_read, 1)

            def empty_attended(place):
                act.wait_ge(attended_done, place.count(lambda i: TILES * i))
                act.copy(sums[:, :], attended[:, 0:CHUNK]).then_inc(attended_free, 1)

            for _, kind, arg in turn_uses(-1):
                use_turn(Place(-1), kind, lambda i: arg, 0, arg[1] if kind in ("q_k", "values") else None)

            def step(place, u):
                k, static = place.k, place.reg is None
                g = STEPS * k + u
                act.wait_ge(scores_full, place.count(lambda i: STEPS * i + u + 1))
                if u % 2 == 0 and not (static and k == 0 and u < EXPS):
                    act.wait_ge(attended_done, place.count(lambda i: (STEPS * i + u) // 2 - EXPS // 2 + 1))
                both = [scores[:, g % 2, :, 0:CHUNK], exps[:, g % EXPS].rearrange("p j h n -> p j (h n)")]
                if u in GP_STEPS:
                    act.activation(both[1], both[0], ACT.Exp, scale=SCALE * SLOPE)
                    if not (static and k == 0 and products(u) < COLDS):
                        act.wait_ge(products_ready, place.count(lambda i: products(STEPS * i + u) - COLDS + 1))
                    act.activation(factors[:, products(g) % COLDS].rearrange("p j h n -> p j (h n)"), both[0],
                                   ACT.Exp, scale=SCALE * (1 - SLOPE)).then_inc(exps_done, 1)
                else:
                    act.activation(both[1], both[0], ACT.Exp, scale=SCALE)
                    if not (static and k == 0 and maxima(u) < COLDS):
                        act.wait_ge(probs_ready, place.count(lambda i: maxima(STEPS * i + u) - COLDS + 1))
                    act.activation(colds[:, maxima(g) % COLDS].rearrange("p j h n -> p j (h n)"), both[0],
                                   ACT.Exp, scale=SCALE * SLOPE).then_inc(exps_done, 1)
                if u == LAG - 1 and not (static and k == 0):
                    empty_attended(place)
                for s, kind, arg in turn_uses(k + (LOOPED if not static else 0)):
                    if s == u:
                        if kind in ("q_k", "values"):
                            use_turn(place, kind, lambda i: (i // CPG + 1, arg[1]), k + CPG, arg[1])
                        else:
                            use_turn(place, kind, lambda i: i // CPG + 1, k + CPG, None)

            walk(act, step)
            empty_attended(Place(CHUNKS))

        @block.vector
        def _(ve):
            ve.memset(values[:, :, :, :, :], 0.0).then_inc(consts_ve, 1)
            ve.wait_ge(consts_ve, 1)
            ve.memset(values[:, :, :, :, D:D + 1], 1.0).then_inc(consts_ve, 1)
            ve.memset(shift_parts[:, :, :], 0.0).then_inc(consts_ve, 1)

            def top_of(place, ahead, v):
                t, h, chunk = v // HEADS, v % HEADS, place.k + ahead
                c = chunk % CPG
                if h == 0:
                    ve.wait_ge(mask_ready, place.count(lambda i: CT * (i + ahead) + t + 1))
                if v == 0 and not (place.reg is None and chunk < 2):
                    ve.wait_ge(shift_ready, place.count(lambda i: i + ahead - 1))
                ve.wait_ge(turn_full, place.count(lambda i: use_no["top", (i + ahead, v)]))
                place.apart(ve)
                banks = scores_banks if place.reg is None and in_scores((chunk, v)) else turn
                ve.tensor_tensor_reduce(
                    out=masked_out[:, int(banks is not turn), :].rearrange("p (a m) -> p a m", a=CPG),
                    in0=banks[0:TILE, 0:CPG, 0:CHUNK],
                    in1=mask[:, c, t, :].rearrange("p (a m) -> p a m", a=CPG), scale=1.0, scalar=LOWEST,
                    op0=ALU.add, op1=ALU.max, accum_out=top[:, chunk % 2, t, h:h + 1]).then_inc(turn_read, 1)

            def rest_of(place, g_of, a):
                ve.wait_ge(part1_ready, place.count(lambda i: 2 * g_of(i) + a + 1))
                for odd in range(2):
                    last = ve.tensor_tensor(in_pairs(rest, a)[:, odd], pairs_in_turn[:, odd],
                                            in_pairs(part1, a)[:, odd], ALU.subtract)
                last.then_inc(turn_read, 1)

            def finish(place):
                ve.wait_ge(turn_full, place.count(lambda i: use_no["finish", i - 1]))
                both = turn[0:TILE, 0, :].rearrange("p (t h d) -> p t h d", t=CT, h=HEADS)
                ve.tensor_scalar(floor_z[:, :, :], both[:, :, :, D], 1e-30, None, ALU.max).then_inc(norm_z, 1)
                ve.wait_ge(norm_z, place.count(lambda i: 2 * (i - 1) + 1))
                ve.reciprocal(recip_z[:, :, :], floor_z[:, :, :]).then_inc(norm_z, 1)
                ve.wait_ge(norm_z, place.count(lambda i: 2 * (i - 1) + 2))
                ve.tensor_tensor(hidden[:, :, :].rearrange("p t (h d) -> p (t h) d", h=HEADS),
                                 turn[0:TILE, 0, :].rearrange("p (t d) -> p t d", d=32)[:, :, 0:D],
                                 recip_z[:, :, :].rearrange("p t (h a) -> p (t h) a", a=1).to_broadcast(
                                     [TILE, CT * HEADS, D]),
                                 ALU.mult).then_inc(turn_read, 1)

            def statistics(place):
                ve.wait_ge(hidden_ready, place.count(lambda i: i))
                for t in range(CT):
                    last = ve.bn_stats(stats[:, t, :], hidden[:, t, :])
                last.then_inc(stats_step, 1)
                ve.wait_ge(stats_step, place.count(lambda i: i))
                place.apart(ve)
                for t in range(CT):
                    last = ve.bn_aggr(moments[:, t, :], stats[:, t, :])
                last.then_inc(stats_ready, 1)

            def transpose_shifts(place, ahead):
                ve.wait_ge(shift_ready, place.count(lambda i: i + ahead + 1))
                place.apart(ve)
                ve.transpose(shift_blocks[:, :, :].rearrange("p t r -> p (t r)"),
                             shift_parts[:, :, :].rearrange("p t r -> p (t r)")).then_inc(blocks_ready, 1)

            for a in range(2):
                rest_of(Place(0), lambda i: 0, a)
            ve.wait_ge(consts_gp, 8)
            for p in range(2):
                ve.tensor_copy(k_stack[PARTS:ROWS, p], own_head[PARTS:ROWS, :].rearrange(
                    "r (h a) -> r h a", a=1).to_broadcast([3 * HEADS, HEADS, N])).then_inc(consts_ve, 1)
            for _, kind, arg in turn_uses(-1):
                if kind == "top":
                    top_of(Place(0), arg[0], arg[1])
                if arg == (0, CT * HEADS - 1):
                    transpose_shifts(Place(0), 0)

            def step(place, u):
                k, static = place.k, place.reg is None
                for s, kind, arg in turn_uses(k + (LOOPED if not static else 0)):
                    if s == u and kind == "top":
                        top_of(place, 1 if top_step(arg[1]) >= 0 else 2, arg[1])
                    elif s == u and kind == "q_k":
                        rest_of(place, lambda i: i // CPG + 1, arg[1])
                    elif s == u and kind == "finish":
                        finish(place)
                if u == 13 and not (static and k == 0):
                    statistics(place)
                if u == 15 and (not static or k + 1 < CHUNKS):
                    transpose_shifts(place, 1)
                if u not in GP_STEPS:
                    g = STEPS * k + u
                    ve.wait_ge(exps_done, place.count(lambda i: STEPS * i + u + 1))
                    ve.tensor_tensor(exps[:, g % EXPS].rearrange("p j h n -> p (j h n)"),
                                     exps[:, g % EXPS].rearrange("p j h n -> p (j h n)"),
                                     colds[:, maxima(g) % COLDS].rearrange("p j h n -> p (j h n)"),
                                     ALU.max).then_inc(probs_ready, 1)

            walk(ve, step)
            ve.wait_ge(normed_ready, CHUNKS - 1)
            finish(Place(CHUNKS))
            statistics(Place(CHUNKS))

        @block.tensor
        def _(pe):
            def product_in_turn(place, kind, arg_of, no_of, v, k):
                early = place.reg is None and kind == "top" and (k, v) in early_tops[1:]
                if not (place.reg is None and no_of(place.k) == 1):
                    pe.wait_ge(turn_read, place.count(lambda i: no_of(i) - (2 if early else 1)))
                if kind == "x_t":
                    pe.wait_ge(x_landed, place.count(lambda i: 16 * (arg_of(i) + 1)))
                    place.apart(pe)
                    for q in range(TILES // 2):
                        last = pe.transpose(turn[:, q // PAIRS, (q % PAIRS) * TILE:(q % PAIRS + 1) * TILE],
                                            x_in[:, 2 * q:2 * q + 2, :].rearrange("p b f -> p (b f)"),
                                            eye[0:TILE, 0:TILE])
                elif kind == "q_k":
                    pe.wait_ge(turn_read, place.count(lambda i: use_no["x_t", arg_of(i)]))
                    for odd in range(2):
                        half = slice(odd * F, (odd + 1) * F)
                        last = pe.matmul(turn[:, odd, 0:PAIRS * TILE],
                                         w_scores[half, :, :, :].rearrange("f a h d -> f (a h d)"),
                                         x_t[half, v * PAIRS:(v + 1) * PAIRS, :].rearrange("f q n -> f (q n)"),
                                         start=True, stop=True)
                elif kind == "values":
                    for q in range(VALUE_PAIRS):
                        for odd in range(2):
                            half = slice(odd * F, (odd + 1) * F)
                            last = pe.matmul(turn[0:TILE, odd, q * F:(q + 1) * F], x_t[half, v * VALUE_PAIRS + q, :],
                                             w_values[half, :, :].rearrange("f h d -> f (h d)"),
                                             start=True, stop=True)
                elif kind == "top":
                    t, h = v // HEADS, v % HEADS
                    if t == 0:
                        pe.wait_ge(stacks_landed[h], place.count(lambda i: 16 * 12 * (arg_of(i) // CPG + 1)))
                    n0 = (k % CPG) * CHUNK + t * TILE
                    banks = scores_banks if place.reg is None and in_scores((k, v)) else turn
                    for a in range(CPG):
                        last = pe.matmul(banks[0:TILE, a, 0:CHUNK], q_stack[0:PARTS, par(k), h, n0:n0 + TILE],
                                         k_stack[0:PARTS, par(k), h, a * CHUNK:(a + 1) * CHUNK],
                                         start=True, stop=True)
                elif kind == "finish":
                    pe.wait_ge(attended_free, place.count(lambda i: arg_of(i) + 1))
                    place.apart(pe)
                    for t in range(CT):
                        last = pe.transpose(turn[0:TILE, 0, t * 128:(t + 1) * 128], sums[:, t * TILE:(t + 1) * TILE],
                                            eye[:, :])
                last.then_inc(turn_full, 1)

            def attend(place, mt):
                k = place.k
                pe.wait_ge(probs_ready, place.count(lambda i: maxima(STEPS * i + 2 * mt + 2)))
                if 2 * mt in GP_STEPS or 2 * mt + 1 in GP_STEPS:
                    pe.wait_ge(products_ready, place.count(lambda i: products(STEPS * i + 2 * mt + 2)))
                if mt == 0 and not (place.reg is None and k == 0):
                    pe.wait_ge(attended_free, place.count(lambda i: i))
                for h in range(HEADS):
                    g = STEPS * k + 2 * mt + h // 2
                    last = pe.matmul(attended[32 * h:32 * h + 32, 0:CHUNK], values[:, par(k), mt, h, :],
                                     exps[:, g % EXPS, :, h % 2, :], start=mt == 0, stop=mt == TILES - 1,
                                     skip_group_check=True)
                last.then_inc(attended_done, 1)

            pe.wait_ge(weights_in, 16 * 7)
            pe.wait_ge(consts_gp, 8)
            pe.wait_ge(consts_ve, 3)
            for _, kind, arg in turn_uses(-1):
                chunk, v = arg if kind in ("top", "q_k", "values") else (arg, None)
                product_in_turn(Place(0), kind, lambda i: chunk, use(kind, lambda i: arg), v, chunk)

            def step(place, u):
                k, static = place.k, place.reg is None
                g, mt, pair = STEPS * k + u, u // 2, u % 2
                c, p = k % CPG, par(k)
                if u == 0:
                    pe.wait_ge(mask_ready, place.count(lambda i: CT * (i + 1)))
                    pe.wait_ge(shifts_landed, place.count(lambda i: 16 * 4 * HEADS * (i + 1)))
                if static and g == 0:
                    pe.wait_ge(consts_ve, 5)
                    pe.wait_ge(turn_read, max(use_no["top", arg] for arg in early_tops if in_scores(arg)))
                if not (static and k == 0 and u < 2):
                    pe.wait_ge(exps_done, place.count(lambda i: STEPS * i + u - 1))
                m = slice(mt * TILE, (mt + 1) * TILE)
                for j in range(2):
                    for s in range(2):
                        pe.matmul(scores[:, g % 2, j, 0:CHUNK].rearrange("m (h n) -> m h n", h=2)[
                                      :, :, s * TILE:(s + 1) * TILE],
                                  mask[:, c, 2 * j + s, m], eye_pair[:, :, :], start=s == 0, stop=False,
                                  skip_group_check=True)
                    for hp in range(2):
                        h, n0 = 2 * pair + hp, c * CHUNK + j * HALF
                        last = pe.matmul(scores[:, g % 2, j, hp * HALF:(hp + 1) * HALF], k_stack[:, p, h, m],
                                         q_stack[:, p, h, n0:n0 + HALF], start=False, stop=True,
                                         skip_group_check=True)
                last.then_inc(scores_full, 1)
                if u % 2 == 0:
                    if u >= LAG:
                        attend(place, mt - LAG // 2)
                    elif not (static and k == 0):
                        attend(Place(k - 1, place.reg), TILES + mt - LAG // 2)
                for s, kind, arg in turn_uses(k + (LOOPED if not static else 0)):
                    if s != u:
                        continue
                    if kind == "top":
                        v = arg[1]
                        ahead = 1 if top_step(v) >= 0 else 2
                        product_in_turn(place, kind, lambda i: i + ahead, lambda i: use_no["top", (i + ahead, v)], v,
                                        k + ahead)
                    elif kind == "finish":
                        product_in_turn(place, kind, lambda i: i - 1, lambda i: use_no["finish", i - 1], None, k)
                    elif kind in ("q_k", "values"):
                        product_in_turn(place, kind, lambda i: i // CPG + 1,
                                        lambda i, kind=kind: use_no[kind, (i // CPG + 1, arg[1])], arg[1], k + CPG)
                    else:
                        product_in_turn(place, kind, lambda i: i // CPG + 1,
                                        lambda i, kind=kind: use_no[kind, i // CPG + 1], None, k + CPG)

            walk(pe, step)
            for mt in range(TILES - LAG // 2, TILES):
                attend(Place(CHUNKS - 1), mt)
            product_in_turn(Place(CHUNKS), "finish", lambda i: i - 1, lambda i: use_no["finish", i - 1], None, CHUNKS)


_INS = ['x', 'adj', 'L0_gnn_kernel', 'L0_gnn_attention_kernel', 'L0_gnn_attention_kernel_2', 'L0_gnn_bias']


def kernel(**inputs):
    import numpy as _np
    import concourse.bacc as _bacc
    from concourse import mybir as _mybir
    from concourse.bass_utils import run_bass_kernel_spmd as _run

    nc = _bacc.Bacc("TRN2", target_bir_lowering=False, num_devices=1)
    arrays, args = {}, []
    for name in _INS:
        a = _np.ascontiguousarray(inputs[name])
        arrays[f"in_{name}_dram"] = a
        args.append(nc.dram_tensor(f"in_{name}_dram", a.shape, _mybir.dt.from_np(a.dtype), kind="ExternalInput").ap())
    shape = tuple(inputs['x'].shape)
    args.append(nc.dram_tensor("out_0_dram", shape, _mybir.dt.float32, kind="ExternalOutput").ap())
    graph_attention_resnorm(nc, *args)
    r = _run(nc, [arrays], core_ids=[0])
    return r.results[0]["out_0_dram"]
```
